# Optimizing a Trainium2 kernel written in Bass

```python
import numpy as np
import jax
import jax.numpy as jnp

def _softmax(x, axis=-1):
    return jax.nn.softmax(x, axis=axis)

def _gelu(x):
    return jax.nn.gelu(x, approximate=True)

def _silu(x):
    return jax.nn.silu(x)

def _sigmoid(x):
    return jax.nn.sigmoid(x)

def _layernorm(x, axis=-1, eps=1e-05):
    m = jnp.mean(x, axis=axis, keepdims=True)
    v = jnp.var(x, axis=axis, keepdims=True)
    return (x - m) / jnp.sqrt(v + eps)

def _scatter_add(tgt, idx, src, axis=0):
    return tgt.at[idx].add(src)

def _segment_sum(src, seg, n):
    return jax.ops.segment_sum(src, seg, n)
kernel_name = 'mk_xattn_ffn_d1_seqx_r4_768578'

def setup_inputs(seed: int=0):
    np.random.seed(seed)
    _w = jnp.asarray

    def _rec_inputs():
        import jax
        import jax.numpy as jnp
        _rk = jax.random.key(seed)
        x = -0.0002928 + 1 * jax.random.normal(jax.random.fold_in(_rk, 1), (4, 512, 256), jnp.float32)
        _lenS = 512 - jax.random.randint(jax.random.fold_in(_rk, 7), (4,), 0, max(1, 512 // 4) + 1, jnp.int32)
        _lenS2 = 512 - jax.random.randint(jax.random.fold_in(_rk, 8), (4,), 0, max(1, 512 // 4) + 1, jnp.int32)
        _ctx_1024P = jax.random.normal(jax.random.fold_in(_rk, 11), (4, 16, 256), jnp.float32)
        _ctx_1024c = jax.random.dirichlet(jax.random.fold_in(_rk, 511), 0.3 * jnp.ones((16,), jnp.float32), (4, 512))
        _ctx_1024t = jnp.einsum('bsk,bkd->bsd', _ctx_1024c, _ctx_1024P)
        _ctx_1024t = _ctx_1024t * jax.lax.rsqrt(jnp.mean(jnp.square(_ctx_1024t)) + 1e-12) * 0.953939
        ctx_1024 = -1.39393e-06 + 0.999914 * (_ctx_1024t + 0.3 * jax.random.normal(jax.random.fold_in(_rk, 611), (4, 512, 256), jnp.float32))
        return (x, ctx_1024)
    x, ctx_1024 = _rec_inputs()

    def _L0_xattn_setup():
        import jax, jax.numpy as jnp
        import numpy as np
        H = 16
        D_MODEL = 256
        D_K = D_MODEL // H

        def _split_heads(x, B, S):
            return x.reshape(B, S, H, D_K).transpose(0, 2, 1, 3)
        key = jax.random.key(seed)
        ks = jax.random.split(key, 11)
        B, S, D = (2, 512, D_MODEL)
        sc = 1.0 / np.sqrt(D)
        return {'query': jax.random.normal(ks[0], (B, S, D), jnp.float32), 'key': jax.random.normal(ks[1], (B, S, D), jnp.float32), 'value': jax.random.normal(ks[2], (B, S, D), jnp.float32), 'Wq': jax.random.normal(ks[3], (D, D), jnp.float32) * sc, 'bq': jnp.zeros((D,), jnp.float32), 'Wk': jax.random.normal(ks[4], (D, D), jnp.float32) * sc, 'bk': jnp.zeros((D,), jnp.float32), 'Wv': jax.random.normal(ks[5], (D, D), jnp.float32) * sc, 'bv': jnp.zeros((D,), jnp.float32), 'Wo': jax.random.normal(ks[6], (D, D), jnp.float32) * sc, 'bo': jnp.zeros((D,), jnp.float32)}
    _L0_xattn_all = _L0_xattn_setup()
    _L0_xattn_in = {k: v for k, v in _L0_xattn_all.items() if k in ('Wq', 'bq', 'Wk', 'bk', 'Wv', 'bv', 'Wo', 'bo')}
    del _L0_xattn_all

    def _L0_ffn_setup():
        import jax, jax.numpy as jnp
        import numpy as np
        EPS = 1e-05
        HEADS = 8
        DIM_KEY = 128
        K = 16
        NUM_KEYS = 64
        key = jax.random.key(seed)
        ks = jax.random.split(key, 5)
        B, T, D = (1, 256, 256)
        x = jax.random.normal(ks[0], (B, T, D), dtype=jnp.float32)
        norm_w = jnp.ones((D,), dtype=jnp.float32)
        wq = jax.random.normal(ks[1], (D, DIM_KEY * HEADS * 2), dtype=jnp.float32) * 0.02
        keys = jax.random.normal(ks[2], (HEADS, NUM_KEYS, 2, DIM_KEY), dtype=jnp.float32) * 0.02
        expert_down = jax.random.normal(ks[3], (NUM_KEYS * NUM_KEYS, D), dtype=jnp.float32) * 0.02
        expert_up = jax.random.normal(ks[4], (NUM_KEYS * NUM_KEYS, D), dtype=jnp.float32) * 0.02
        return {'x': x, 'norm_w': norm_w, 'wq': wq, 'keys': keys, 'expert_down': expert_down, 'expert_up': expert_up}
    _L0_ffn_all = _L0_ffn_setup()
    _L0_ffn_in = {k: v for k, v in _L0_ffn_all.items() if k in ('norm_w', 'wq', 'keys', 'expert_down', 'expert_up')}
    del _L0_ffn_all
    return {'x': x, 'ctx_1024': ctx_1024, 'L0_xattn_Wq': _L0_xattn_in['Wq'], 'L0_xattn_bq': _L0_xattn_in['bq'], 'L0_xattn_Wk': _L0_xattn_in['Wk'], 'L0_xattn_bk': _L0_xattn_in['bk'], 'L0_xattn_Wv': _L0_xattn_in['Wv'], 'L0_xattn_bv': _L0_xattn_in['bv'], 'L0_xattn_Wo': _L0_xattn_in['Wo'], 'L0_xattn_bo': _L0_xattn_in['bo'], 'L0_ffn_norm_w': _L0_ffn_in['norm_w'], 'L0_ffn_wq': _L0_ffn_in['wq'], 'L0_ffn_keys': _L0_ffn_in['keys'], 'L0_ffn_expert_down': _L0_ffn_in['expert_down'], 'L0_ffn_expert_up': _L0_ffn_in['expert_up']}

def reference(x, ctx_1024, L0_xattn_Wq, L0_xattn_bq, L0_xattn_Wk, L0_xattn_bk, L0_xattn_Wv, L0_xattn_bv, L0_xattn_Wo, L0_xattn_bo, L0_ffn_norm_w, L0_ffn_wq, L0_ffn_keys, L0_ffn_expert_down, L0_ffn_expert_up):
    import jax
    import jax.numpy as jnp

    def _L0_xattn_ref(query, key, value, Wq, bq, Wk, bk, Wv, bv, Wo, bo):
        import jax, jax.numpy as jnp
        import numpy as np
        H = 16
        D_MODEL = 256
        D_K = D_MODEL // H

        def _split_heads(x, B, S):
            return x.reshape(B, S, H, D_K).transpose(0, 2, 1, 3)
        B, S, D = query.shape
        q = _split_heads(query @ Wq + bq, B, S)
        k = _split_heads(key @ Wk + bk, B, key.shape[1])
        v = _split_heads(value @ Wv + bv, B, value.shape[1])
        scores = jnp.einsum('bhqd,bhkd->bhqk', q, k) / jnp.sqrt(jnp.asarray(D_K, q.dtype))
        p_attn = jax.nn.softmax(scores, axis=-1)
        x = jnp.einsum('bhqk,bhkd->bhqd', p_attn, v)
        x = x.transpose(0, 2, 1, 3).reshape(B, S, H * D_K)
        return x @ Wo + bo

    def _L0_ffn_ref(x, norm_w, wq, keys, expert_down, expert_up):
        import jax, jax.numpy as jnp
        import numpy as np
        EPS = 1e-05
        HEADS = 8
        DIM_KEY = 128
        K = 16
        NUM_KEYS = 64
        B, T, D = x.shape
        inv = jax.lax.rsqrt(jnp.mean(x * x, axis=-1, keepdims=True) + EPS)
        x_norm = x * inv * norm_w
        q = (x_norm @ wq).reshape(B, T, HEADS, 2, DIM_KEY)
        sim = jnp.einsum('bthpd,hkpd->pbthk', q, keys)
        s1, i1 = jax.lax.top_k(sim[0], K)
        s2, i2 = jax.lax.top_k(sim[1], K)
        all_idx = (i1[..., :, None] * NUM_KEYS + i2[..., None, :]).reshape(B, T, HEADS, K * K)
        all_scores = (s1[..., :, None] + s2[..., None, :]).reshape(B, T, HEADS, K * K)
        final_scores, pk = jax.lax.top_k(all_scores, K)
        final_idx = jnp.take_along_axis(all_idx, pk, axis=-1)
        wd = expert_down[final_idx]
        wu = expert_up[final_idx]
        hidden = jnp.einsum('btd,bthkd->bthk', x_norm, wd)
        hidden = jax.nn.gelu(hidden, approximate=False)
        hidden = hidden * jax.nn.relu(final_scores)
        out = jnp.einsum('bthk,bthkd->btd', hidden, wu)
        return out
    x = x + _L0_xattn_ref(_layernorm(x, axis=-1), ctx_1024, ctx_1024, L0_xattn_Wq, L0_xattn_bq, L0_xattn_Wk, L0_xattn_bk, L0_xattn_Wv, L0_xattn_bv, L0_xattn_Wo, L0_xattn_bo)
    x = x + _L0_ffn_ref(_layernorm(x, axis=-1), L0_ffn_norm_w, L0_ffn_wq, L0_ffn_keys, L0_ffn_expert_down, L0_ffn_expert_up)
    return x

_drawn_inputs = setup_inputs


def setup_inputs(seed=0):
    import zlib

    import numpy as np

    out = dict(_drawn_inputs(seed))
    spreads = {'L0_xattn_bq': (0.0, 0.382),
     'L0_xattn_bk': (0.0, 0.8),
     'L0_xattn_bv': (0.0, 0.1),
     'L0_xattn_bo': (0.0, 0.1),
     'L0_ffn_norm_w': (1.0, 0.6)}
    factors = {'L0_ffn_wq': 5.106,
     'L0_ffn_keys': 5.09,
     'L0_ffn_expert_down': 5.131,
     'L0_ffn_expert_up': 5.021}
    for name, (base, spread) in spreads.items():
        noise = np.random.default_rng([zlib.crc32(name.encode()), seed]).standard_normal(out[name].shape)
        drawn = base * np.exp(spread * noise) if base else spread * noise
        out[name] = jnp.asarray(drawn.astype(out[name].dtype))
    for name, factor in factors.items():
        out[name] = (out[name] * factor).astype(out[name].dtype)
    return out
```

```python
import numpy as np
import concourse.bass as bass
from concourse import mybir
from contextlib import ExitStack

F32 = mybir.dt.float32
BF16 = mybir.dt.bfloat16
I32 = mybir.dt.int32
U32 = mybir.dt.uint32
ALU = mybir.AluOpType
ACT = mybir.ActivationFunctionType
AX = mybir.AxisListType

B, S, D = 4, 512, 256
NT = B * S
P = 128
KD = D // P
H, DK = 16, 16
HG = 4
NG = B * H // HG
TB = S // P
NSLOT = 6
QPART = (0, 0, 1, 1, 0, 2)
KPART = (0, 1, 0, 1, 2, 0)
SK = NSLOT * DK
MR = 2
EPS = 1e-5
FH, NK, TOPK = 8, 64, 16
NE = NK * NK
HP = FH * 2
JL = NE // P
TILES = NT // P
CH = 2
TC = CH * P
TK = 16
BPT = P // TK
ROWS = [TOPK // (a + 1) for a in range(TOPK)]
NC = sum(ROWS)
SEGS = []
for _a, _n in enumerate(ROWS):
    if SEGS and SEGS[-1][2] == _n:
        SEGS[-1] = (SEGS[-1][0], SEGS[-1][1] + 1, _n, SEGS[-1][3])
    else:
        SEGS.append((_a, 1, _n, sum(ROWS[:_a])))
GONE = float(np.float32(-3.0e38))
PBITS, LOW = 25, 6


class Arena:

    def __init__(self, tensor, words):
        self.tensor, self.words, self.at = tensor, words, 0

    def take(self, words, dt=F32):
        a = self.at
        self.at += (words + 7) // 8 * 8
        assert self.at <= self.words, self.at
        v = self.tensor[:, a:a + words]
        return v if dt == F32 else v.bitcast(dt)


def build(nc, x, ctx_in, Wq, bq, Wk, bk, Wv, bv, Wo, bo, norm_w, wq, keys, down, up, out):
    ctx = ExitStack()
    with ctx:
        def sem(name):
            return ctx.enter_context(nc.semaphore(name))

        parts_d = nc.dram_tensor("parts_d", (B, 2, 3, D, S), BF16, kind="Internal").ap()
        mrow_d = nc.dram_tensor("mrow_d", (NG, MR * HG, S), BF16, kind="Internal").ap()
        x1_d = nc.dram_tensor("x1_d", (NT, D), F32, kind="Internal").ap()
        xn_d = nc.dram_tensor("xn_d", (P, KD, NT), F32, kind="Internal").ap()

        WORDS = 53200
        mem = Arena(ctx.enter_context(nc.sbuf_tensor("mem", [P, WORDS], F32)), WORDS)
        psum = [ctx.enter_context(nc.psum_tensor(f"bank{i}", [P, 512], F32)) for i in range(8)]

        downT = mem.take(KD * JL * P).rearrange("p (k j e) -> p k j e", k=KD, j=JL)
        wqk = mem.take(KD * HP * NK).rearrange("p (k n) -> p k n", k=KD)
        identf = mem.take(P)
        identb = mem.take(P // 2, BF16)
        mark = mem.at

        x_sb = [mem.take(TB * D).rearrange("p (t d) -> p t d", t=TB) for _ in range(3)]
        c_sb = [mem.take(TB * D).rearrange("p (t d) -> p t d", t=TB) for _ in range(2)]
        xn_sb = mem.take(TB * D).rearrange("p (t d) -> p t d", t=TB)
        xT = mem.take(KD * S).rearrange("p (k t) -> p k t", k=KD)
        cT = mem.take(KD * S).rearrange("p (k t) -> p k t", k=KD)
        proj = [mem.take(S) for _ in range(2)]
        rest = mem.take(S)
        part = [mem.take(3 * S // 2, BF16).rearrange("p (c t) -> p c t", c=3) for _ in range(2)]
        qst = [mem.take(HG * S // 2, BF16).rearrange("p (h t) -> p h t", h=HG) for _ in range(4)]
        kst = [mem.take(HG * S // 2, BF16).rearrange("p (h t) -> p h t", h=HG) for _ in range(4)]
        v_sb = [mem.take(TB * H * 32).rearrange("p (t h c) -> p t h c", t=TB, h=H) for _ in range(2)]
        p_sb = [mem.take(HG * S).rearrange("p (h t) -> p h t", h=HG) for _ in range(3)]
        oT = [mem.take(S) for _ in range(2)]
        attn = mem.take(TB * D).rearrange("p (t d) -> p t d", t=TB)
        aT = mem.take(KD * S).rearrange("p (k t) -> p k t", k=KD)
        x1 = [mem.take(CH * D).rearrange("p (t d) -> p t d", t=CH) for _ in range(2)]
        y_sb = [mem.take(CH * D).rearrange("p (t d) -> p t d", t=CH) for _ in range(2)]
        xnT = [mem.take(KD * TC).rearrange("p (k t) -> p k t", k=KD) for _ in range(2)]
        w_sb = [mem.take(KD * D).rearrange("p (k n) -> p k n", k=KD) for _ in range(4)]
        Wq_sb, Wk_sb, Wv_sb, Wo_sb = w_sb
        bqk = mem.take(2 * KD).rearrange("p (w k) -> p w k", w=2)
        nw = mem.take(KD)
        brow = mem.take(2 * D)
        ones = mem.take(P)
        nmx = [mem.take(TB * HG).rearrange("p (t h) -> p t h", t=TB) for _ in range(2)]
        mres = mem.take(TB * HG).rearrange("p (t h) -> p t h", t=TB)
        mpart = [mem.take(TB * MR * HG // 2, BF16).rearrange("p (t c h) -> p t c h", t=TB, c=MR) for _ in range(2)]
        mrow = [mem.take(S // 2, BF16) for _ in range(2)]
        rden = mem.take(TB * HG).rearrange("p (t h) -> p t h", t=TB)
        st6 = mem.take(TB * 6).rearrange("p (t c) -> p t c", t=TB)
        mv = mem.take(TB * 2).rearrange("p (t c) -> p t c", t=TB)
        rstd = [mem.take(TB) for _ in range(2)]
        half = mem.take(TB)
        st6e = mem.take(CH * 6).rearrange("p (t c) -> p t c", t=CH)
        mve = mem.take(CH * 2).rearrange("p (t c) -> p t c", t=CH)
        chain = [mem.take(CH) for _ in range(6)]
        dn_sb = [mem.take(2 * D).rearrange("p (j d) -> p j d", j=2) for _ in range(2)]
        wq_sb = [mem.take(KD * 2 * P).rearrange("p (k n) -> p k n", k=KD) for _ in range(2)]
        ky_sb = [mem.take(2 * P).rearrange("p (c d) -> p c d", c=2) for _ in range(2)]
        wqT = mem.take(2 * KD * P).rearrange("p (c k f) -> p c k f", c=2, k=KD)
        kyT = mem.take(2 * NK).rearrange("p (c n) -> p c n", c=2)

        mem.at = mark
        up_sb = mem.take(JL * D).rearrange("p (j d) -> p j d", j=JL)
        iota = mem.take(P * TK // 2, BF16).rearrange("p (c t) -> p c t", c=P)
        coef = [mem.take(JL * TC).rearrange("p (j t) -> p j t", j=JL) for _ in range(2)]
        xs = [mem.take(KD * P).rearrange("p (k t) -> p k t", k=KD) for _ in range(2)]
        xm = [mem.take(KD * TC).rearrange("p (k t) -> p k t", k=KD) for _ in range(2)]
        sim = [mem.take(HP * NK) for _ in range(2)]
        oh = [mem.take(P * TK // 2, BF16).rearrange("p (c t) -> p c t", c=P) for _ in range(2)]
        oj = [mem.take(JL * TK // 2, BF16).rearrange("p (c t) -> p c t", c=JL) for _ in range(2)]
        ow = [mem.take(3 * JL * TK // 2, BF16).rearrange("p (w c t) -> p w c t", w=3, c=JL) for _ in range(2)]
        gm = [mem.take(2 * TC).rearrange("p (j t) -> p j t", j=2) for _ in range(4)]
        s16 = [mem.take(HP * TOPK).rearrange("p (h c n) -> p h c n", h=FH, c=2) for _ in range(2)]
        i16 = [mem.take(HP * TOPK, U32).rearrange("p (h c n) -> p h c n", h=FH, c=2) for _ in range(2)]
        i64 = mem.take(FH * TOPK, I32).rearrange("p (h n) -> p h n", h=FH)
        gate = mem.take(2)
        one = mem.take(1)
        k64 = mem.take(1, I32)
        left = [mem.take(NK) for _ in range(2)]
        cand, c1, wkey, ikey = (mem.take(FH * NC).rearrange("p (h n) -> p h n", h=FH) for _ in range(4))
        cidx = mem.take(FH * NC, I32).rearrange("p (h n) -> p h n", h=FH)
        pcode = mem.take(FH * NC, I32).rearrange("p (h n) -> p h n", h=FH)
        best = mem.take(FH * 16).rearrange("p (h n) -> p h n", h=FH)
        kA, kB = (mem.take(FH * TOPK).rearrange("p (h n) -> p h n", h=FH) for _ in range(2))
        wA, wB, eH, eL = (mem.take(P, I32) for _ in range(4))
        wf = [mem.take(P) for _ in range(2)]
        wres = mem.take(P)
        tok = [mem.take(5 * P // 2, BF16).rearrange("p (c n) -> p c n", c=5) for _ in range(2)]
        tokT = [mem.take(5 * P // 2, BF16).rearrange("p (c t) -> p c t", c=5) for _ in range(2)]
        outT = mem.take(KD * TC).rearrange("p (k t) -> p k t", k=KD)
        xr = mem.take(CH * D).rearrange("p (t d) -> p t d", t=CH)

        SLOTS = NG + 4
        before = [(0, "xT", (0, 0)), (0, "xT", (0, 1)), (0, "cT", (0, 0)), (0, "cT", (0, 1)), (0, "proj", (0, 0)),
                  (0, "proj", (0, 1)), (0, "proj", (0, 2)), (0, "proj", (0, 3)), (0, "v", (0, 0)), (0, "v", (0, 1))]
        plan = []
        for g in range(SLOTS):
            b, r = g // HG, g % HG
            ev = []
            if 1 <= g <= NG:
                ev.append((1, "max", g - 1))
            if 3 <= g < NG + 3:
                ev.append((4, "oT", g - 3))
            if r == 0 and b + 1 < B:
                ev += [(11, "xT", (b + 1, 0)), (12, "xT", (b + 1, 1)), (13, "cT", (b + 1, 0)), (14, "cT", (b + 1, 1))]
            if r == 1 and b + 1 < B:
                ev += [(2 + 3 * n, "proj", (b + 1, n)) for n in range(4)]
            if r == 2 and b + 1 < B:
                ev += [(3, "v", (b + 1, 0)), (5, "v", (b + 1, 1))]
            if r == 2 and b >= 1:
                ev += [(8, "aT", (b - 1, 0)), (9, "aT", (b - 1, 1)), (12, "o", (b - 1, 0)), (14, "o", (b - 1, 1))]
            if r == 3 and b >= 1:
                ev += [(6, "yT", (b - 1, 0)), (8, "yT", (b - 1, 1))]
            if g < JL // 2:
                ev.append((7, "down", g))
            if g < HP // 2:
                ev += [(9, "wqT", g), (10, "kyT", g), (15, "wqk", g)]
            plan.append(sorted(ev, key=lambda e: e[0]))
        order = {(n, i): e for e, (_, n, i) in enumerate(before + [e for s in plan for e in s])}

        misc_full = [sem("misc_full0"), sem("misc_full1")]
        misc_read = [sem("misc_read0"), sem("misc_read1")]

        def place(name, index):
            e = order[(name, index)]
            return e % 2, e // 2, psum[6 + e % 2]

        def wait_taken(eng, name, index):
            bank, n, _ = place(name, index)
            eng.wait_ge(misc_read[bank], n + 1)

        def wait_filled(eng, name, index):
            bank, n, ps = place(name, index)
            eng.wait_ge(misc_full[bank], n + 1)
            return ps, misc_read[bank]

        consts = sem("consts")
        w_ld = sem("w_ld")
        x_ld = [sem(f"x_ld{i}") for i in range(3)]
        c_ld = [sem(f"c_ld{i}") for i in range(2)]
        ln_stat = sem("ln_stat")
        ln_rstd = sem("ln_rstd")
        ln_out = sem("ln_out")
        split = sem("split")
        part_wr = [sem(f"part_wr{i}") for i in range(4)]
        st_ld = [sem(f"st_ld{i}") for i in range(4)]
        mr_wr = [sem(f"mr_wr{i}") for i in range(2)]
        mr_ld = [sem(f"mr_ld{i}") for i in range(4)]
        s_full = sem("s_full")
        s_max = sem("s_max")
        mp_done = sem("mp_done")
        t_full = sem("t_full")
        p_ready = sem("p_ready")
        pv_done = sem("pv_done")
        o_ev = sem("o_ev")
        nrm = sem("nrm")
        e_stat = sem("e_stat")
        e_scale = sem("e_scale")
        e_fin = sem("e_fin")
        e_out = sem("e_out")
        x1_wr = [sem(f"x1_wr{i}") for i in range(2)]
        xn_wr = [sem(f"xn_wr{i}") for i in range(2)]
        dn_ld = [sem(f"dn_ld{i}") for i in range(2)]
        wq_ld = [sem(f"wq_ld{i}") for i in range(2)]
        phase = sem("phase")

        HBN = 8

        up_ld = sem("up_ld")
        econst = sem("econst")
        pcd = sem("pcd")
        xs_ld = [sem(f"xs_ld{i}") for i in range(2)]
        xm_ld = [sem(f"xm_ld{i}") for i in range(2)]
        xr_ld = sem("xr_ld")
        sim_mm = sem("sim_mm")
        sim_ev = sem("sim_ev")
        dve_step = sem("dve_step")
        pool_step = sem("pool_step")
        st1 = sem("st1")
        cix = sem("cix")
        key = sem("key")
        dec_w = sem("dec_w")
        dec = sem("dec")
        wsp = sem("wsp")
        tok_mm = sem("tok_mm")
        tok_ev = sem("tok_ev")
        oh_rdy = sem("oh_rdy")
        ow_rdy = sem("ow_rdy")
        c_mm = sem("c_mm")
        c_ev = sem("c_ev")
        g_mm = sem("g_mm")
        g_act = sem("g_act")
        m_rdy = sem("m_rdy")
        o_mm = sem("o_mm")
        ot_ev = sem("ot_ev")
        fin_mm = sem("fin_mm")
        fin_add = sem("fin_add")
        out_wr = sem("out_wr")

        def at_least(eng, s, value):
            if isinstance(value, int) and value <= 0:
                return
            eng.wait_ge(s, value)

        class Steps:

            def __init__(self, eng, s):
                self.eng, self.s, self.n = eng, s, 0

            def count(self, instruction):
                instruction.then_inc(self.s, 1)
                self.n += 1
                return self.n

            def after(self, n):
                self.eng.wait_ge(self.s, n)

            def all(self):
                if self.n:
                    self.after(self.n)

            def restart(self):
                if self.n:
                    self.after(self.n)
                    self.eng.sem_clear(self.s)
                    self.n = 0

        HALVES = 2
        FIRST, LAST = 3, 6

        def slots(eng, body):
            for k in range(FIRST):
                body(k, k % 2, k)
            with eng.Fori(0, (LAST - FIRST + 1) // 2) as i:
                for j in range(2):
                    body(i * 2 + (FIRST + j), (FIRST + j) % 2, None)
            for k in range(LAST + 1, 11):
                body(k, k % 2, k)

        def on(k, lo, hi):
            return k is None or lo <= k <= hi

        def back(k, par, kk, q, lag):
            q -= lag
            if q >= 0:
                return k, par, kk, q
            return k - 1, 1 - par, None if kk is None else kk - 1, q + 16

        block = ctx.enter_context(nc.Block())

        @block.sync
        def _(sp):
            for w, src in zip(w_sb, (Wq, Wk, Wv, Wo)):
                sp.dma_start(w, src.rearrange("(k p) n -> p k n", p=P)).then_inc(w_ld, 16)
            for n, src in enumerate((bq, bk)):
                for k in range(KD):
                    sp.dma_start(bqk[:, n, k:k + 1], src[k * P:(k + 1) * P].rearrange("(p o) -> p o", o=1)).then_inc(w_ld, 16)
            for k in range(KD):
                sp.dma_start(nw[:, k:k + 1], norm_w[k * P:(k + 1) * P].rearrange("(p o) -> p o", o=1)).then_inc(w_ld, 16)
            for n, src in enumerate((bv, bo)):
                sp.dma_start(brow[0:1, n * D:(n + 1) * D], src.rearrange("(o n) -> o n", o=1)).then_inc(w_ld, 16)

            def load_x(b):
                if b >= 3:
                    wait_taken(sp, "o", (b - 3, 1))
                sp.dma_start(x_sb[b % 3], x[b].rearrange("(t p) d -> p t d", p=P)).then_inc(x_ld[b % 3], 16)
                if b >= 2:
                    wait_taken(sp, "cT", (b - 2, 1))
                sp.dma_start(c_sb[b % 2], ctx_in[b].rearrange("(t p) d -> p t d", p=P)).then_inc(c_ld[b % 2], 16)

            def store_parts(b, n):
                sp.wait_ge(split, 4 * (4 * b + n + 1))
                dst = parts_d[b, n % 2, :, (n // 2) * P:(n // 2 + 1) * P, :].rearrange("c p t -> p c t")
                sp.dma_start(dst, part[n % 2]).then_inc(part_wr[n], 16)

            def load_stacks(g):
                b, r = g // HG, g % HG
                for n in (2 * (r // 2), 2 * (r // 2) + 1):
                    sp.wait_ge(part_wr[n], 16 * (b + 1))
                if g >= 4:
                    sp.wait_ge(pv_done, 4 * (g - 3))
                for w, (dst, pick) in enumerate(((qst, QPART), (kst, KPART))):
                    for s, c in enumerate(pick):
                        src = parts_d[b, w, c, r * HG * DK:(r + 1) * HG * DK, :].rearrange("(h d) t -> d h t", d=DK)
                        sp.dma_start(dst[g % 4][s * DK:(s + 1) * DK], src).then_inc(st_ld[g % 4], 16)

            def relay_max(g):
                wait_taken(sp, "max", g)
                sp.dma_start(mrow_d[g], mrow[g % 2][0:MR * HG, :]).then_inc(mr_wr[g % 2], 16)
                sp.wait_ge(mr_wr[g % 2], 16 * (g // 2 + 1))
                sp.dma_start(qst[g % 4][SK:SK + MR], mrow_d[g].rearrange("(c h) t -> c h t", c=MR)).then_inc(mr_ld[g % 4], 16)

            def load_setup(n):
                if n < JL // 2:
                    if n >= 2:
                        wait_taken(sp, "down", n - 2)
                    src = down.rearrange("(p j) d -> p j d", j=JL)
                    sp.dma_start(dn_sb[n % 2], src[:, 2 * n:2 * n + 2, :]).then_inc(dn_ld[n % 2], 16)
                if n < HP // 2:
                    if n >= 2:
                        wait_taken(sp, "kyT", n - 2)
                    sp.dma_start(wq_sb[n % 2], wq.rearrange("(k p) n -> p k n", p=P)[:, :, n * 2 * P:(n + 1) * 2 * P])\
                      .then_inc(wq_ld[n % 2], 16)
                    sp.dma_start(ky_sb[n % 2][0:NK], keys[n]).then_inc(wq_ld[n % 2], 16)

            def store_half(b, e):
                n = 2 * b + e
                rows = slice(b * S + e * TC, b * S + (e + 1) * TC)
                sp.wait_ge(e_out, 2 * (n + 1))
                sp.dma_start(x1_d[rows, :].rearrange("(t p) d -> p t d", p=P), x1[e]).then_inc(x1_wr[e], 16)
                wait_taken(sp, "yT", (b, e))
                sp.dma_start(xn_d[:, :, rows], xnT[e]).then_inc(xn_wr[e], 16)

            load_x(0)
            load_x(1)
            load_setup(0)
            load_setup(1)
            for n in range(4):
                store_parts(0, n)
            load_stacks(0)
            for g in range(SLOTS):
                b, r = g // HG, g % HG
                if 1 <= g <= NG:
                    relay_max(g - 1)
                if g + 1 < NG:
                    load_stacks(g + 1)
                if r == 3 and b + 2 < B:
                    load_x(b + 2)
                load_setup(g + 2)
                if r == 1 and b + 1 < B:
                    for n in range(4):
                        store_parts(b + 1, n)
                if r == 3 and b >= 1:
                    store_half(b - 1, 0)
                    store_half(b - 1, 1)
            for s in (*x1_wr, *xn_wr):
                sp.wait_ge(s, 16 * B)
            sp.sem_inc(phase, 1)
            sp.wait_ge(phase, 5)

            sp.dma_start(up_sb, up.rearrange("(p j) d -> p j d", j=JL)).then_inc(up_ld, 16)

            def load_sim_input(tile, parity):
                at_least(sp, sim_mm, (tile - 1) * 2)
                sp.dma_start(xs[parity], xn_d[:, :, bass.ds(tile * P, P)]).then_inc(xs_ld[parity], 16)

            load_sim_input(0, 0)
            load_sim_input(1, 1)

            def body(k, par, kk):
                if on(kk, 3, 10):
                    sp.dma_start(xr, x1_d[bass.ds((k - 3) * TC, TC), :].rearrange("(t p) d -> p t d", p=P))\
                      .then_inc(xr_ld, 16)
                if on(kk, 1, 8):
                    at_least(sp, g_mm, (k - 2) * 16)
                    sp.dma_start(xm[1 - par], xn_d[:, :, bass.ds((k - 1) * TC, TC)]).then_inc(xm_ld[1 - par], 16)
                if on(kk, 3, 10):
                    sp.wait_ge(fin_add, k - 2)
                    dst = out.rearrange("b s d -> (b s) d")[bass.ds((k - 3) * TC, TC), :]
                    sp.dma_start(dst.rearrange("(t p) d -> p t d", p=P), xr).then_inc(out_wr, 16)
                    sp.wait_ge(out_wr, (k - 2) * 16)
                for hf in range(HALVES):
                    if on(kk, 0, 6):
                        load_sim_input(k * 2 + hf + 2, hf)

            slots(sp, body)

        @block.gpsimd
        def _(pool):
            nc.gpsimd.memset(identf, 0.0).then_inc(consts, 1)
            nc.gpsimd.memset(ones, 1.0).then_inc(consts, 1)
            nc.gpsimd.memset(half, -0.5).then_inc(consts, 1)
            pool.wait_ge(consts, 3)
            nc.gpsimd.affine_select(out=identf, in_=identf, compare_op=ALU.not_equal, fill=1.0, base=0,
                                    pattern=[[-1, P]], channel_multiplier=1).then_inc(consts, 1)
            pool.wait_ge(consts, 4)
            nc.gpsimd.tensor_copy(identb, identf).then_inc(consts, 1)
            for i in range(4):
                pool.wait_ge(consts, 5 + i)
                nc.gpsimd.memset(kst[i][SK:SK + MR], 1.0).then_inc(consts, 1)
            pool.wait_ge(consts, 9)
            for i in range(2):
                nc.gpsimd.memset(v_sb[i], 1.0).then_inc(consts, 1)

            def first_rstd(b):
                pool.wait_ge(ln_stat, 8 * (b + 1))
                nc.gpsimd.tensor_scalar(rstd[0], mv[:, :, 1], EPS, None, ALU.add).then_inc(ln_rstd, 1)
                pool.wait_ge(ln_rstd, 2 * b + 1)
                nc.gpsimd.tensor_tensor(rstd[1], rstd[0], half, ALU.pow).then_inc(ln_rstd, 1)

            def split_projection(b, n):
                e = 4 * b + n
                f, c = proj[n % 2], part[n % 2]
                wait_taken(pool, "proj", (b, n))
                if b or n >= 2:
                    pool.wait_ge(part_wr[(n + 2) % 4], 16 * (b if n < 2 else b + 1))
                nc.gpsimd.tensor_copy(c[:, 0, :], f).then_inc(split, 1)
                pool.wait_ge(split, 4 * e + 1)
                nc.gpsimd.tensor_tensor(rest, f, c[:, 0, :], ALU.subtract).then_inc(split, 1)
                pool.wait_ge(split, 4 * e + 2)
                nc.gpsimd.tensor_copy(c[:, 1, :], rest).then_inc(split, 1)
                pool.wait_ge(split, 4 * e + 3)
                nc.gpsimd.tensor_tensor(c[:, 2, :], rest, c[:, 1, :], ALU.subtract).then_inc(split, 1)

            def second_scale(n):
                a, r, v1, v2, v3, s2 = chain
                base = 6 * n
                pool.wait_ge(e_stat, 4 * (n + 1))
                if n:
                    pool.wait_ge(e_out, 2 * n)
                nc.gpsimd.tensor_scalar(a, mve[:, :, 1], EPS, None, ALU.add).then_inc(e_scale, 1)
                pool.wait_ge(e_scale, base + 1)
                nc.gpsimd.tensor_tensor(r, a, half[:, 0:CH], ALU.pow).then_inc(e_scale, 1)
                pool.wait_ge(e_scale, base + 2)
                nc.gpsimd.tensor_tensor(v1, mve[:, :, 1], r, ALU.mult).then_inc(e_scale, 1)
                pool.wait_ge(e_scale, base + 3)
                nc.gpsimd.tensor_tensor(v2, v1, r, ALU.mult).then_inc(e_scale, 1)
                pool.wait_ge(e_scale, base + 4)
                nc.gpsimd.tensor_scalar(v3, v2, EPS, None, ALU.add).then_inc(e_scale, 1)
                pool.wait_ge(e_scale, base + 5)
                nc.gpsimd.tensor_tensor(v2, v3, half[:, 0:CH], ALU.pow).then_inc(e_scale, 1)
                pool.wait_ge(e_scale, base + 6)
                nc.gpsimd.tensor_tensor(s2, v2, r, ALU.mult).then_inc(e_fin, 1)

            first_rstd(0)
            for n in range(4):
                split_projection(0, n)
            for g in range(SLOTS):
                b, r = g // HG, g % HG
                if r == 0 and b + 1 < B:
                    first_rstd(b + 1)
                if r == 1 and b + 1 < B:
                    for n in range(4):
                        split_projection(b + 1, n)
                if r == 2 and b >= 1:
                    second_scale(2 * (b - 1))
                    second_scale(2 * (b - 1) + 1)
            pool.wait_ge(e_fin, 2 * B)
            pool.sem_inc(phase, 1)
            pool.wait_ge(phase, 5)

            nc.gpsimd.memset(k64, NK).then_inc(econst, 1)
            nc.gpsimd.memset(gate, 0.0).then_inc(econst, 1)
            nc.gpsimd.memset(one, 1.0).then_inc(econst, 1)
            nc.gpsimd.iota(pcode, pattern=[[0, FH], [1, NC]], base=8, channel_multiplier=0).then_inc(econst, 1)
            numbers = coef[0].rearrange("p j t -> p (j t)")[:, 0:P * TK].bitcast(I32).rearrange("p (c t) -> p c t", c=P)
            nc.gpsimd.iota(numbers, pattern=[[1, P], [0, TK]], base=0, channel_multiplier=0).then_inc(econst, 1)
            pool.wait_ge(econst, 5)
            nc.gpsimd.tensor_copy(iota, numbers).then_inc(econst, 1)

            steps = Steps(pool, pool_step)

            def candidate_numbers(u, hf):
                at_least(pool, st1, (u + 1) * FH)
                at_least(pool, key, u)
                if isinstance(u, int) and u == 0:
                    pool.wait_ge(pcd, 1)
                steps.all()
                ii = i16[hf].bitcast(I32)
                n0 = steps.count(nc.gpsimd.tensor_tensor(i64, ii[:, :, 0, :], k64.unsqueeze(2).to_broadcast([P, FH, TOPK]),
                                                         ALU.mult))
                steps.after(n0)
                for a, rows, n, at in SEGS:
                    o = cidx[:, :, at:at + rows * n].rearrange("p h (a b) -> p h a b", a=rows)
                    i0 = i64[:, :, a:a + rows].unsqueeze(3).to_broadcast([P, FH, rows, n])
                    i1 = ii[:, :, 1, 0:n].unsqueeze(2).to_broadcast([P, FH, rows, n])
                    if rows == 1:
                        o, i0, i1 = o[:, :, 0, :], i0[:, :, 0, :], i1[:, :, 0, :]
                    steps.count(nc.gpsimd.tensor_tensor(o, i0, i1, ALU.add))
                steps.all()
                nc.gpsimd.tensor_tensor(cidx, cidx, pcode, ALU.add).then_inc(cix, 1)

            def weight_parts(v, hf):
                w, c = wf[hf], tok[hf]
                pool.wait_ge(dec_w, v + 1)
                at_least(pool, tok_mm, v - 1)
                steps.all()
                n = steps.count(nc.gpsimd.tensor_tensor(c[:, 2, :], w, one.to_broadcast([P, P]), ALU.mult))
                steps.after(n)
                n = steps.count(nc.gpsimd.tensor_tensor(wres, w, c[:, 2, :], ALU.subtract))
                steps.after(n)
                n = steps.count(nc.gpsimd.tensor_copy(c[:, 3, :], wres))
                steps.after(n)
                nc.gpsimd.tensor_tensor(c[:, 4, :], wres, c[:, 3, :], ALU.subtract).then_inc(wsp, 1)

            def weigh(c, q):
                pool.wait_ge(oh_rdy, c * 2 + 2)
                at_least(pool, c_mm, c - 1)
                i0 = oj[q % 2].unsqueeze(1).to_broadcast([P, 3, JL, TK])
                t0 = q % BPT * TK
                i1 = tokT[q // BPT][:, 2:5, t0:t0 + TK].unsqueeze(2).to_broadcast([P, 3, JL, TK])
                nc.gpsimd.tensor_tensor(ow[q % 2], i0, i1, ALU.mult).then_inc(ow_rdy, 1)

            def body(k, par, kk):
                steps.restart()
                for hf in range(HALVES):
                    u = k * 2 + hf
                    if on(kk, 1, 8):
                        for s in range(BPT):
                            weigh((k - 1) * 16 + (hf * BPT + s), hf * BPT + s)
                    if on(kk, 1, 7) or (kk, hf) in ((0, 1), (8, 0)):
                        weight_parts(u - 1, 1 - hf)
                    if on(kk, 0, 7):
                        candidate_numbers(u, hf)

            slots(pool, body)

        @block.scalar
        def _(act):
            act.wait_ge(w_ld, 12 * 16)

            def take(name, index):
                if name in ("o", "oT"):
                    return
                ps, done = wait_filled(act, name, index)
                if name in ("xT", "cT"):
                    b, e = index
                    dst = xT if name == "xT" else cT
                    src = ps[:, :].rearrange("p (k t) -> p k t", k=KD)
                    nc.scalar.copy(dst[:, :, e * TC:(e + 1) * TC], src).then_inc(done, 1)
                elif name == "proj":
                    b, n = index
                    if b or n >= 2:
                        act.wait_ge(split, 4 * (4 * b + n - 1))
                    nc.scalar.activation(proj[n % 2], ps[:, :], ACT.Identity, bias=bqk[:, n % 2, n // 2:n // 2 + 1])\
                      .then_inc(done, 1)
                elif name == "v":
                    b, e = index
                    if b >= 2:
                        act.wait_ge(pv_done, 16 * (b - 1))
                    if b < 2 and e == 0:
                        act.wait_ge(consts, 11)
                    src = ps[:, :].rearrange("p (t h c) -> p t h c", t=CH, h=H)
                    for t in range(CH):
                        i = nc.scalar.copy(v_sb[b % 2][:, e * CH + t, :, 0:DK], src[:, t])
                    i.then_inc(done, 1)
                elif name == "max":
                    if index >= 2:
                        act.wait_ge(mr_wr[index % 2], 16 * (index // 2))
                    nc.scalar.copy(mrow[index % 2][0:MR * HG, :], ps[0:MR * HG, 0:S // 2].bitcast(BF16)).then_inc(done, 1)
                elif name == "aT":
                    b, e = index
                    src = ps[:, :].rearrange("p (k t) -> p k t", k=KD)
                    nc.scalar.copy(aT[:, :, e * TC:(e + 1) * TC], src).then_inc(done, 1)
                elif name == "yT":
                    b, e = index
                    if b >= 1:
                        act.wait_ge(xn_wr[e], 16 * b)
                    src = ps[:, :].rearrange("p (k t) -> p k t", k=KD)
                    for c in range(KD):
                        i = nc.scalar.activation(xnT[e][:, c, :], src[:, c, :], ACT.Copy, scale=nw[:, c:c + 1])
                    i.then_inc(done, 1)
                elif name == "down":
                    src = ps[:, :].rearrange("p (k j e) -> p k j e", k=KD, j=2)
                    for c in range(KD):
                        i = nc.scalar.copy(downT[:, c, 2 * index:2 * index + 2, :], src[:, c])
                    i.then_inc(done, 1)
                elif name == "wqT":
                    if index >= 1:
                        wait_taken(act, "wqk", index - 1)
                    nc.scalar.copy(wqT, ps[:, :].rearrange("p (c k f) -> p c k f", c=2, k=KD)).then_inc(done, 1)
                elif name == "kyT":
                    nc.scalar.copy(kyT, ps[:, 0:2 * NK].rearrange("p (c n) -> p c n", c=2)).then_inc(done, 1)
                elif name == "wqk":
                    src = ps[:, 0:KD * 2 * NK].rearrange("p (k n) -> p k n", k=KD)
                    nc.scalar.copy(wqk[:, :, index * 2 * NK:(index + 1) * 2 * NK], src).then_inc(done, 1)
                else:
                    raise ValueError(name)

            def probabilities(g, i):
                n = 16 * g + i
                quad, hh = 4 * g + i // HG, i % HG
                act.wait_ge(t_full, n + 1)
                if quad >= 3 and hh == 0:
                    act.wait_ge(pv_done, quad - 2)
                nc.scalar.activation(p_sb[quad % 3][:, hh, :], psum[3 + n % 2][:, :], ACT.Exp, scale=DK ** -0.5)\
                  .then_inc(p_ready, 1)

            for _, name, index in before:
                take(name, index)
            for g in range(SLOTS):
                for i in range(16):
                    if 2 <= g < NG + 2:
                        probabilities(g - 2, i)
                    if i == 2 and 3 <= g < NG + 3:
                        act.wait_ge(pv_done, 4 * (g - 2))
                        if g >= 5:
                            bank, n, _ = place("oT", g - 5)
                            act.wait_ge(misc_full[bank], n + 1)
                        nc.scalar.copy(oT[(g - 3) % 2], psum[5][:, :]).then_inc(o_ev, 1)
                    for _, name, index in [e for e in plan[g] if e[0] == i]:
                        take(name, index)
            wait_taken(act, "yT", (B - 1, 1))
            act.sem_inc(phase, 1)
            act.wait_ge(phase, 5)

            def take_sim(u, hf, n):
                act.wait_ge(sim_mm, u * 2 + (n + 1))
                at_least(act, st1, (u - 1) * FH)
                nc.scalar.copy(sim[hf][:, n * 512:(n + 1) * 512], psum[n][:, :]).then_inc(sim_ev, 1)

            def take_tok(w, hf):
                act.wait_ge(tok_mm, w + 1)
                at_least(act, ow_rdy, (w - 1) * BPT)
                at_least(act, oh_rdy, (w - 1) * BPT * 2)
                nc.scalar.copy(tokT[hf], psum[0][:, 0:5 * P // 2].bitcast(BF16).rearrange("p (c t) -> p c t", c=5))\
                  .then_inc(tok_ev, 1)

            def gelu(g, q):
                act.wait_ge(g_mm, g + 1)
                at_least(act, o_mm, g - 3)
                nc.scalar.activation(gm[q % 4], psum[4 + q % 2][:, :].rearrange("p (j t) -> p j t", j=2), ACT.Gelu)\
                  .then_inc(g_act, 1)

            def take_coef(k, par, q):
                act.wait_ge(c_mm, (k - 1) * 16 + (q + 1))
                if q == 0:
                    at_least(act, m_rdy, (k - 2) * 16)
                src = psum[2 + q % 2][:, :].rearrange("p (t j) -> p j t", j=JL)
                nc.scalar.copy(coef[1 - par][:, :, q * TK:(q + 1) * TK], src).then_inc(c_ev, 1)

            def take_out(k):
                act.wait_ge(o_mm, (k - 2) * 16)
                for c in range(KD):
                    i = nc.scalar.copy(outT[:, c, :], psum[6 + c][:, 0:TC])
                i.then_inc(ot_ev, 1)

            take_sim(0, 0, 0)
            take_sim(0, 0, 1)

            def body(k, par, kk):
                for q in range(16):
                    hf, s = q // BPT, q % BPT
                    u = k * 2 + hf
                    if s == 0 and on(kk, 1, 8):
                        take_tok(u - 2, hf)
                    if on(kk, 2, 9):
                        gelu((k - 2) * 16 + q, q)
                    k1, p1, kk1, q1 = back(k, par, kk, q, 1)
                    if on(kk1, 1, 8):
                        take_coef(k1, p1, q1)
                    if q == 2 and on(kk, 3, 10):
                        take_out(k)
                    if s in (5, 6) and (on(kk, 0, 6) or (kk, hf) == (7, 0)):
                        take_sim(u + 1, 1 - hf, s - 5)

            slots(act, body)

        @block.vector
        def _(dve):
            def first_norm(b):
                xb = x_sb[b % 3]
                dve.wait_ge(x_ld[b % 3], 16 * (b // 3 + 1))
                for t in range(TB):
                    nc.vector.bn_stats(st6[:, t, :], xb[:, t, :]).then_inc(ln_stat, 1)
                if b:
                    dve.wait_ge(ln_rstd, 2 * b)
                for t in range(TB):
                    dve.wait_ge(ln_stat, 8 * b + t + 1)
                    nc.vector.bn_aggr(mv[:, t, :], st6[:, t, :]).then_inc(ln_stat, 1)

            def first_norm_apply(b):
                dve.wait_ge(ln_rstd, 2 * (b + 1))
                dve.wait_ge(ln_stat, 8 * (b + 1))
                if b:
                    wait_filled(dve, "xT", (b - 1, 1))
                for t in range(TB):
                    nc.vector.tensor_scalar(xn_sb[:, t, :], x_sb[b % 3][:, t, :], mv[:, t, 0:1], rstd[1][:, t:t + 1],
                                            ALU.subtract, ALU.mult).then_inc(ln_out, 1)

            def max_parts(g):
                m, n = mpart[g % 2], nmx[g % 2]
                dve.wait_ge(s_max, 16 * (g + 1))
                if g >= 2:
                    wait_filled(dve, "max", g - 2)
                nc.vector.tensor_copy(m[:, :, 0, :], n).then_inc(mp_done, 1)
                dve.wait_ge(mp_done, 3 * g + 1)
                nc.vector.tensor_tensor(mres, n, m[:, :, 0, :], ALU.subtract).then_inc(mp_done, 1)
                dve.wait_ge(mp_done, 3 * g + 2)
                nc.vector.tensor_copy(m[:, :, 1, :], mres).then_inc(mp_done, 1)

            def normalise(g):
                ps, done = wait_filled(dve, "oT", g)
                if g >= 4 and g % 4 == 0:
                    wait_filled(dve, "aT", (g // 4 - 1, 1))
                v = ps[:, :].rearrange("p (t h c) -> p t h c", t=TB, h=HG)
                if g:
                    wait_taken(dve, "oT", g - 1)
                nc.vector.reciprocal(rden, v[:, :, :, DK]).then_inc(nrm, 1)
                dve.wait_ge(nrm, g + 1)
                r = g % HG
                o = attn[:, :, r * HG * DK:(r + 1) * HG * DK].rearrange("p t (h c) -> p t h c", h=HG)
                nc.vector.tensor_tensor(o, v[:, :, :, 0:DK], rden.unsqueeze(3).to_broadcast([P, TB, HG, DK]), ALU.mult)\
                  .then_inc(done, 1)

            def residual(b, e):
                n = 2 * b + e
                ps, done = wait_filled(dve, "o", (b, e))
                if b:
                    dve.wait_ge(x1_wr[e], 16 * b)
                nc.vector.tensor_tensor(x1[e], ps[:, :].rearrange("p (t d) -> p t d", t=CH),
                                        x_sb[b % 3][:, e * CH:(e + 1) * CH, :], ALU.add).then_inc(done, 1)
                wait_taken(dve, "o", (b, e))
                for t in range(CH):
                    nc.vector.bn_stats(st6e[:, t, :], x1[e][:, t, :]).then_inc(e_stat, 1)
                if n:
                    dve.wait_ge(e_fin, n)
                for t in range(CH):
                    dve.wait_ge(e_stat, 4 * n + t + 1)
                    nc.vector.bn_aggr(mve[:, t, :], st6e[:, t, :]).then_inc(e_stat, 1)

            def second_norm(b, e):
                n = 2 * b + e
                dve.wait_ge(e_fin, n + 1)
                dve.wait_ge(e_stat, 4 * (n + 1))
                if b:
                    wait_filled(dve, "yT", (b - 1, e))
                for t in range(CH):
                    nc.vector.tensor_scalar(y_sb[e][:, t, :], x1[e][:, t, :], mve[:, t, 0:1], chain[5][:, t:t + 1],
                                            ALU.subtract, ALU.mult).then_inc(e_out, 1)

            first_norm(0)
            first_norm_apply(0)
            for g in range(SLOTS):
                b, r = g // HG, g % HG
                for i in range(16):
                    if i == 0 and 1 <= g <= NG:
                        max_parts(g - 1)
                    if g < NG:
                        n = 16 * g + i
                        dve.wait_ge(s_full, n + 1)
                        nc.vector.tensor_reduce(nmx[g % 2][:, i % TB, i // TB:i // TB + 1], psum[n % 3][:, :], AX.X,
                                                ALU.max, negate=True).then_inc(s_max, 1)
                    if i == 3 and r == 0 and b + 1 < B:
                        first_norm(b + 1)
                    if i == 8 and r == 0 and b + 1 < B:
                        first_norm_apply(b + 1)
                    if i == 4 and 3 <= g < NG + 3:
                        normalise(g - 3)
                    if r == 2 and b >= 1 and i in (12, 14):
                        residual(b - 1, (i - 12) // 2)
                    if r == 2 and b >= 1 and i in (13, 15):
                        second_norm(b - 1, (i - 13) // 2)
            dve.wait_ge(e_out, 4 * B)
            dve.sem_inc(phase, 1)
            dve.wait_ge(phase, 5)

            dve.wait_ge(econst, 4)
            nc.vector.tensor_scalar(pcode, pcode, PBITS, None, ALU.logical_shift_left).then_inc(pcd, 1)

            def bits(ap):
                return ap.bitcast(I32)

            steps = Steps(dve, dve_step)

            def search(hf, h):
                s, i = s16[hf], i16[hf]
                src = [sim[hf][:, (2 * h + c) * NK:(2 * h + c + 1) * NK] for c in range(2)]
                top = [steps.count(nc.vector.max(s[:, h, c, 0:8], src[c])) for c in range(2)]
                for c in range(2):
                    steps.after(top[c])
                    steps.count(nc.vector.max_index(i[:, h, c, 0:8], s[:, h, c, 0:8], src[c]))
                cut = [steps.count(nc.vector.match_replace(left[c], s[:, h, c, 0:8], src[c], GONE)) for c in range(2)]
                top = []
                for c in range(2):
                    steps.after(cut[c])
                    top.append(steps.count(nc.vector.max(s[:, h, c, 8:16], left[c])))
                steps.after(top[0])
                steps.count(nc.vector.max_index(i[:, h, 0, 8:16], s[:, h, 0, 8:16], left[0]))
                steps.after(top[1])
                nc.vector.max_index(i[:, h, 1, 8:16], s[:, h, 1, 8:16], left[1]).then_inc(st1, 1)

            def candidates(hf):
                steps.all()
                s = s16[hf]
                for a, rows, n, at in SEGS:
                    o = cand[:, :, at:at + rows * n].rearrange("p h (a b) -> p h a b", a=rows)
                    i0 = s[:, :, 0, a:a + rows].unsqueeze(3).to_broadcast([P, FH, rows, n])
                    i1 = s[:, :, 1, 0:n].unsqueeze(2).to_broadcast([P, FH, rows, n])
                    if rows == 1:
                        o, i0, i1 = o[:, :, 0, :], i0[:, :, 0, :], i1[:, :, 0, :]
                    steps.count(nc.vector.tensor_tensor(o, i0, i1, ALU.add))

            def choose(s):
                hs = (2 * s, 2 * s + 1)
                if s == 0:
                    steps.all()
                a = [steps.count(nc.vector.max(best[:, h, 0:8], cand[:, h, :])) for h in hs]
                b = []
                for n, h in enumerate(hs):
                    steps.after(a[n])
                    b.append(steps.count(nc.vector.match_replace(c1[:, h, :], best[:, h, 0:8], cand[:, h, :], GONE)))
                c = []
                for n, h in enumerate(hs):
                    steps.after(b[n])
                    c.append(steps.count(nc.vector.max(best[:, h, 8:16], c1[:, h, :])))
                for n, h in enumerate(hs):
                    steps.after(c[n])
                    steps.count(nc.vector.match_replace(c1[:, h, :], best[:, h, 8:16], c1[:, h, :], GONE))

            def make_keys(v):
                w, ik = bits(wkey), bits(ikey)
                relu = steps.count(nc.vector.tensor_scalar(wkey, cand, 0.0, 0.0, ALU.max, ALU.add))
                steps.after(relu)
                low = steps.count(nc.vector.tensor_scalar(ik, w, (1 << LOW) - 1, 12, ALU.bitwise_and,
                                                          ALU.logical_shift_left))
                high = steps.count(nc.vector.scalar_tensor_tensor(w, w, LOW, pcode, ALU.logical_shift_right,
                                                                  ALU.bitwise_or))
                dve.wait_ge(cix, v + 1)
                steps.after(low)
                nc.vector.tensor_tensor(ik, ik, cidx, ALU.bitwise_or).then_inc(key, 1)
                steps.after(high)
                steps.count(nc.vector.scalar_tensor_tensor(wkey, c1, GONE, wkey, ALU.is_equal, ALU.mult))
                dve.wait_ge(key, v + 1)
                steps.count(nc.vector.scalar_tensor_tensor(ikey, c1, GONE, ikey, ALU.is_equal, ALU.mult))

            def extract(s):
                if s == 0:
                    steps.all()
                both = [(k, o, h) for h in (2 * s, 2 * s + 1) for k, o in ((wkey, kA), (ikey, kB))]
                a = [steps.count(nc.vector.max(o[:, h, 0:8], k[:, h, :])) for k, o, h in both]
                b = []
                for n, (k, o, h) in enumerate(both):
                    steps.after(a[n])
                    b.append(steps.count(nc.vector.match_replace(k[:, h, :], o[:, h, 0:8], k[:, h, :], 0.0)))
                for n, (k, o, h) in enumerate(both):
                    steps.after(b[n])
                    steps.count(nc.vector.max(o[:, h, 8:16], k[:, h, :]))

            def decode(v, hf):
                a = bits(kA.rearrange("p h n -> p (h n)"))
                b = bits(kB.rearrange("p h n -> p (h n)"))
                at_least(dve, wsp, v - 1)
                at_least(dve, tok_mm, v - 1)
                steps.all()
                wa = steps.count(nc.vector.tensor_scalar(wA, a, (1 << PBITS) - 1, LOW, ALU.bitwise_and,
                                                         ALU.logical_shift_left))
                wb = steps.count(nc.vector.tensor_scalar(wB, b, 12, (1 << LOW) - 1, ALU.logical_shift_right,
                                                         ALU.bitwise_and))
                eh = steps.count(nc.vector.tensor_scalar(eH, b, NE - 1, 5, ALU.bitwise_and, ALU.logical_shift_right))
                el = steps.count(nc.vector.tensor_scalar(eL, b, JL - 1, None, ALU.bitwise_and))
                steps.after(wb)
                nc.vector.tensor_tensor(bits(wf[hf]), wA, wB, ALU.bitwise_or).then_inc(dec_w, 1)
                steps.after(el)
                steps.count(nc.vector.tensor_copy(tok[hf][:, 0, :], eH))
                nc.vector.tensor_copy(tok[hf][:, 1, :], eL).then_inc(dec, 1)

            def one_hots(c, q):
                at_least(dve, c_mm, c - 1)
                at_least(dve, ow_rdy, c - 1)
                t0 = q % BPT * TK
                tt = tokT[q // BPT]
                nc.vector.tensor_tensor(oj[q % 2], tt[:, 1:2, t0:t0 + TK].to_broadcast([P, JL, TK]), iota[:, 0:JL, :],
                                        ALU.is_equal).then_inc(oh_rdy, 1)
                nc.vector.tensor_tensor(oh[q % 2], tt[:, 0:1, t0:t0 + TK].to_broadcast([P, P, TK]), iota,
                                        ALU.is_equal).then_inc(oh_rdy, 1)

            def weigh_hidden(k, par, q):
                dve.wait_ge(g_act, (k - 2) * 16 + (q + 1))
                if q == 0:
                    dve.wait_ge(c_ev, (k - 1) * 16)
                nc.vector.tensor_tensor(gm[q % 4], gm[q % 4], coef[par][:, 2 * q:2 * q + 2, :], ALU.mult)\
                  .then_inc(m_rdy, 1)

            def add_residual(m):
                dve.wait_ge(fin_mm, m + 1)
                dve.wait_ge(xr_ld, (m + 1) * 16)
                nc.vector.tensor_tensor(xr, psum[1][:, :].rearrange("p (t d) -> p t d", t=CH), xr, ALU.add)\
                  .then_inc(fin_add, 1)

            def body(k, par, kk):
                steps.restart()
                for q in range(16):
                    hf, s = q // BPT, q % BPT
                    u = k * 2 + hf
                    if on(kk, 0, 7):
                        if s == 0:
                            dve.wait_ge(sim_ev, (u + 1) * 2)
                            at_least(dve, cix, u - 1)
                            nc.vector.tensor_copy(gate[:, 0:1], gate[:, 1:2])
                        search(hf, s)
                    k1, p1, kk1, q1 = back(k, par, kk, q, 1)
                    if on(kk1, 2, 9):
                        weigh_hidden(k1, p1, q1)
                    if on(kk, 1, 7) or (kk, hf) in ((0, 1), (8, 0)):
                        if s < 4:
                            choose(s)
                        if s == 4:
                            make_keys(u - 1)
                        if s >= 4:
                            extract(s - 4)
                        if s == 7:
                            decode(u - 1, 1 - hf)
                    if on(kk, 1, 8):
                        if s == 0:
                            dve.wait_ge(tok_ev, u - 1)
                            if kk == 1 and hf == 0:
                                dve.wait_ge(econst, 6)
                        one_hots((k - 1) * 16 + q, q)
                    if q == 4 and on(kk, 3, 10):
                        add_residual(k - 3)
                    if s == 7 and on(kk, 0, 7):
                        candidates(hf)

            slots(dve, body)

        @block.tensor
        def _(pe):
            def mm(o, l, r, first=True, last=True):
                return nc.tensor.matmul(o, l, r, start=first, stop=last)

            def turn(o, i, ident):
                return nc.tensor.transpose(o, i, ident)

            def event(name, index):
                bank, n, ps = place(name, index)
                if n:
                    pe.wait_ge(misc_read[bank], n)
                if name in ("xT", "cT"):
                    b, e = index
                    if name == "xT":
                        pe.wait_ge(ln_out, 4 * (b + 1))
                    else:
                        pe.wait_ge(c_ld[b % 2], 16 * (b // 2 + 1))
                    src = xn_sb if name == "xT" else c_sb[b % 2]
                    for k in range(KD):
                        for t in range(CH):
                            last = turn(ps[:, k * TC + t * P:k * TC + (t + 1) * P],
                                        src[:, e * CH + t, k * P:(k + 1) * P], identf)
                elif name == "proj":
                    b, n4 = index
                    wait_taken(pe, "cT" if n4 % 2 else "xT", (b, 0))
                    wait_taken(pe, "cT" if n4 % 2 else "xT", (b, 1))
                    w, src = (Wk_sb, cT) if n4 % 2 else (Wq_sb, xT)
                    for k in range(KD):
                        last = mm(ps[:, :], w[:, k, n4 // 2 * P:(n4 // 2 + 1) * P], src[:, k, :], k == 0, k == KD - 1)
                elif name == "v":
                    b, e = index
                    wait_taken(pe, "cT", (b, e))
                    for t in range(CH):
                        o = ps[:, t * D:(t + 1) * D]
                        for k in range(KD):
                            mm(o, cT[:, k, (e * CH + t) * P:(e * CH + t + 1) * P], Wv_sb[:, k, :], k == 0, False)
                        last = mm(o, ones[0:1, :], brow[0:1, 0:D], False, True)
                elif name == "max":
                    g = index
                    pe.wait_ge(mp_done, 3 * (g + 1))
                    psb = ps[:, 0:S // 2].bitcast(BF16)
                    for t in range(TB):
                        last = turn(psb[0:MR * HG, t * P:(t + 1) * P], mpart[g % 2][:, t].rearrange("p c h -> p (c h)"), identb)
                elif name == "oT":
                    g = index
                    pe.wait_ge(o_ev, g + 1)
                    for t in range(TB):
                        last = turn(ps[:, t * P:(t + 1) * P], oT[g % 2][:, t * P:(t + 1) * P], identf)
                elif name == "aT":
                    b, e = index
                    wait_taken(pe, "oT", HG * b + 2)
                    wait_taken(pe, "oT", HG * b + 3)
                    for k in range(KD):
                        for t in range(CH):
                            last = turn(ps[:, k * TC + t * P:k * TC + (t + 1) * P],
                                        attn[:, e * CH + t, k * P:(k + 1) * P], identf)
                elif name == "o":
                    b, e = index
                    wait_taken(pe, "aT", (b, e))
                    for t in range(CH):
                        o = ps[:, t * D:(t + 1) * D]
                        for k in range(KD):
                            mm(o, aT[:, k, (e * CH + t) * P:(e * CH + t + 1) * P], Wo_sb[:, k, :], k == 0, False)
                        last = mm(o, ones[0:1, :], brow[0:1, D:2 * D], False, True)
                elif name == "yT":
                    b, e = index
                    pe.wait_ge(e_out, 2 * (2 * b + e + 1))
                    for k in range(KD):
                        for t in range(CH):
                            last = turn(ps[:, k * TC + t * P:k * TC + (t + 1) * P], y_sb[e][:, t, k * P:(k + 1) * P], identf)
                elif name == "down":
                    n2 = index
                    pe.wait_ge(dn_ld[n2 % 2], 16 * (n2 // 2 + 1))
                    for k in range(KD):
                        for j in range(2):
                            last = turn(ps[:, (k * 2 + j) * P:(k * 2 + j + 1) * P],
                                        dn_sb[n2 % 2][:, j, k * P:(k + 1) * P], identf)
                elif name == "wqT":
                    n2 = index
                    pe.wait_ge(wq_ld[n2 % 2], 32 * (n2 // 2 + 1))
                    for c in range(2):
                        for k in range(KD):
                            last = turn(ps[:, (c * KD + k) * P:(c * KD + k + 1) * P],
                                        wq_sb[n2 % 2][:, k, c * P:(c + 1) * P], identf)
                elif name == "kyT":
                    n2 = index
                    for c in range(2):
                        last = turn(ps[:, c * NK:(c + 1) * NK], ky_sb[n2 % 2][0:NK, c, :], identf[0:NK, 0:NK])
                elif name == "wqk":
                    wait_taken(pe, "wqT", index)
                    wait_taken(pe, "kyT", index)
                    for k in range(KD):
                        for c in range(2):
                            last = mm(ps[:, (k * 2 + c) * NK:(k * 2 + c + 1) * NK], wqT[:, c, k, :], kyT[:, c, :])
                last.then_inc(misc_full[bank], 1)

            def scores(g, i):
                n = 16 * g + i
                if i == 0:
                    pe.wait_ge(st_ld[g % 4], 2 * NSLOT * 16 * (g // 4 + 1))
                if n >= 3:
                    pe.wait_ge(s_max, n - 2)
                hh, t = i // TB, i % TB
                mm(psum[n % 3][:, :], qst[g % 4][0:SK, hh, t * P:(t + 1) * P], kst[g % 4][0:SK, hh, :]).then_inc(s_full, 1)

            def turned_scores(g, i):
                n = 16 * g + i
                if i == 0:
                    pe.wait_ge(mr_ld[g % 4], 16 * (g // 4 + 1))
                if n >= 2:
                    pe.wait_ge(p_ready, n - 1)
                t, hh = i // HG, i % HG
                mm(psum[3 + n % 2][:, :], kst[g % 4][0:SK + MR, hh, t * P:(t + 1) * P], qst[g % 4][0:SK + MR, hh, :])\
                    .then_inc(t_full, 1)

            def values(quad):
                g, t = quad // TB, quad % TB
                b, r = g // HG, g % HG
                pe.wait_ge(p_ready, 4 * (quad + 1))
                if t == 0:
                    if g:
                        pe.wait_ge(o_ev, g)
                    wait_taken(pe, "v", (b, 0))
                    wait_taken(pe, "v", (b, 1))
                for hh in range(HG):
                    last = mm(psum[5][32 * hh:32 * hh + 32, :], v_sb[b % 2][:, t, r * HG + hh, :], p_sb[quad % 3][:, hh, :],
                              t == 0, t == TB - 1)
                last.then_inc(pv_done, 1)

            pe.wait_ge(consts, 11)
            pe.wait_ge(w_ld, 12 * 16)
            for _, name, index in before:
                event(name, index)
            for g in range(SLOTS):
                for i in range(16):
                    for _, name, index in [e for e in plan[g] if e[0] == i]:
                        event(name, index)
                    if 2 <= g < NG + 2:
                        turned_scores(g - 2, i)
                    if g < NG:
                        scores(g, i)
                    quad = 4 * (g - 2) + i // 4 - 1
                    if i % 4 == 1 and 0 <= quad < 4 * NG:
                        values(quad)
            wait_filled(pe, "yT", (B - 1, 1))
            pe.sem_inc(phase, 1)
            pe.wait_ge(phase, 5)

            def similarities(k, u, hf, n):
                if n == 0:
                    pe.wait_ge(xs_ld[hf], (u - hf) * 8 + 16)
                    at_least(pe, tok_ev, u - 2)
                else:
                    at_least(pe, fin_add, k - 2)
                at_least(pe, sim_ev, u * 2 + (n - 1))
                for k in range(KD):
                    last = mm(psum[n][:, :], xs[hf][:, k, :], wqk[:, k, n * 512:(n + 1) * 512], k == 0, k == KD - 1)
                last.then_inc(sim_mm, 1)

            def turn_numbers(w, hf):
                pe.wait_ge(dec, w + 1)
                pe.wait_ge(wsp, w + 1)
                at_least(pe, sim_ev, min(w * 2 + 5, 31) if isinstance(w, int) else w * 2 + 5)
                psb = psum[0][:, 0:5 * P // 2].bitcast(BF16)
                for c in range(5):
                    last = turn(psb[:, c * P:(c + 1) * P], tok[hf][:, c, :], identb)
                last.then_inc(tok_mm, 1)

            def coefficients(k, q):
                c = (k - 1) * 16 + q
                pe.wait_ge(oh_rdy, c * 2 + 2)
                pe.wait_ge(ow_rdy, c + 1)
                at_least(pe, c_ev, c - 1)
                for t in range(TK):
                    for w in range(3):
                        last = mm(psum[2 + q % 2][:, t * JL:(t + 1) * JL], oh[q % 2][:, :, t], ow[q % 2][:, w, :, t],
                                  w == 0, w == 2)
                last.then_inc(c_mm, 1)

            def hidden(k, par, q):
                g = (k - 2) * 16 + q
                if q == 0:
                    pe.wait_ge(xm_ld[par], (k - par) * 8)
                at_least(pe, g_act, g - 1)
                for j in range(2):
                    for c in range(KD):
                        last = mm(psum[4 + q % 2][:, j * TC:(j + 1) * TC], downT[:, c, 2 * q + j, :], xm[par][:, c, :],
                                  c == 0, c == KD - 1)
                last.then_inc(g_mm, 1)

            def output(k, kk, q):
                g = (k - 2) * 16 + q
                if kk == 2 and q == 0:
                    pe.wait_ge(up_ld, 16)
                if q == 0:
                    at_least(pe, ot_ev, k - 2)
                pe.wait_ge(m_rdy, g + 1)
                for j in range(2):
                    for c in range(KD):
                        last = mm(psum[6 + c][:, 0:TC], up_sb[:, 2 * q + j, c * P:(c + 1) * P], gm[q % 4][:, j, :],
                                  q == 0 and j == 0, q == 15 and j == 1)
                last.then_inc(o_mm, 1)

            def turn_output(k):
                pe.wait_ge(ot_ev, k - 2)
                at_least(pe, sim_ev, min(4 * k + 2, 32) if isinstance(k, int) else k * 4 + 2)
                for t in range(CH):
                    for c in range(KD):
                        last = turn(psum[1][:, t * D + c * P:t * D + (c + 1) * P], outT[:, c, t * P:(t + 1) * P], identf)
                last.then_inc(fin_mm, 1)

            similarities(0, 0, 0, 0)
            similarities(0, 0, 0, 1)

            def body(k, par, kk):
                for q in range(16):
                    hf, s = q // BPT, q % BPT
                    u = k * 2 + hf
                    if s == 0 and on(kk, 1, 8):
                        turn_numbers(u - 2, hf)
                    if on(kk, 2, 9):
                        hidden(k, par, q)
                    k1, p1, kk1, q1 = back(k, par, kk, q, 1)
                    if on(kk1, 1, 8):
                        coefficients(k1, q1)
                    k2, p2, kk2, q2 = back(k, par, kk, q, 2)
                    if on(kk2, 2, 9):
                        output(k2, kk2, q2)
                    if q == 3 and on(kk, 3, 10):
                        turn_output(k)
                    if s in (5, 6) and (on(kk, 0, 6) or (kk, hf) == (7, 0)):
                        similarities(k, u + 1, 1 - hf, s - 5)

            slots(pe, body)


_INS = ["x", "ctx_1024", "L0_xattn_Wq", "L0_xattn_bq", "L0_xattn_Wk", "L0_xattn_bk", "L0_xattn_Wv", "L0_xattn_bv",
        "L0_xattn_Wo", "L0_xattn_bo", "L0_ffn_norm_w", "L0_ffn_wq", "L0_ffn_keys", "L0_ffn_expert_down",
        "L0_ffn_expert_up"]


def kernel(**inputs):
    import concourse.bacc as bacc
    from concourse.bass_utils import run_bass_kernel_spmd

    nc = bacc.Bacc("TRN2", target_bir_lowering=False, num_devices=1)
    arrays, args = {}, []
    for name in _INS:
        a = np.ascontiguousarray(inputs[name])
        arrays[f"in_{name}"] = a
        args.append(nc.dram_tensor(f"in_{name}", a.shape, mybir.dt.from_np(a.dtype), kind="ExternalInput").ap())
    out = nc.dram_tensor("out_0", (B, S, D), F32, kind="ExternalOutput").ap()
    build(nc, *args, out)
    r = run_bass_kernel_spmd(nc, [arrays], core_ids=[0])
    return r.results[0]["out_0"]
```

```python
import numpy as np
import concourse.bass as bass
from concourse import mybir
from contextlib import ExitStack

F32 = mybir.dt.float32
BF16 = mybir.dt.bfloat16
I32 = mybir.dt.int32
U32 = mybir.dt.uint32
ALU = mybir.AluOpType
ACT = mybir.ActivationFunctionType
AX = mybir.AxisListType

B, S, D = 4, 512, 256
NT = B * S
P = 128
KD = D // P
H, DK = 16, 16
HG = 4
NG = B * H // HG
TB = S // P
NSLOT = 6
QPART = (0, 0, 1, 1, 0, 2)
KPART = (0, 1, 0, 1, 2, 0)
SK = NSLOT * DK
MR = 2
EPS = 1e-5
FH, NK, TOPK = 8, 64, 16
NE = NK * NK
HP = FH * 2
JL = NE // P
TILES = NT // P
CH = 2
TC = CH * P
TK = 16
BPT = P // TK
ROWS = [TOPK // (a + 1) for a in range(TOPK)]
NC = sum(ROWS)
SEGS = []
for _a, _n in enumerate(ROWS):
    if SEGS and SEGS[-1][2] == _n:
        SEGS[-1] = (SEGS[-1][0], SEGS[-1][1] + 1, _n, SEGS[-1][3])
    else:
        SEGS.append((_a, 1, _n, sum(ROWS[:_a])))
GONE = float(np.float32(-3.0e38))
PBITS, LOW = 25, 6


class Arena:

    def __init__(self, tensor, words):
        self.tensor, self.words, self.at = tensor, words, 0

    def take(self, words, dt=F32):
        a = self.at
        self.at += (words + 7) // 8 * 8
        assert self.at <= self.words, self.at
        v = self.tensor[:, a:a + words]
        return v if dt == F32 else v.bitcast(dt)


def build(nc, x, ctx_in, Wq, bq, Wk, bk, Wv, bv, Wo, bo, norm_w, wq, keys, down, up, out):
    ctx = ExitStack()
    with ctx:
        def sem(name):
            return ctx.enter_context(nc.semaphore(name))

        parts_d = nc.dram_tensor("parts_d", (B, 2, 3, D, S), BF16, kind="Internal").ap()
        mrow_d = nc.dram_tensor("mrow_d", (NG, MR * HG, S), BF16, kind="Internal").ap()
        x1_d = nc.dram_tensor("x1_d", (NT, D), F32, kind="Internal").ap()
        xn_d = nc.dram_tensor("xn_d", (P, KD, NT + P), F32, kind="Internal").ap()
        downT_d = nc.dram_tensor("downT_d", (P, KD, JL, P), F32, kind="Internal").ap()
        tok_d = nc.dram_tensor("tok_d", (TILES * P, 5 * P), BF16, kind="Internal").ap()

        WORDS = 53200
        mem = Arena(ctx.enter_context(nc.sbuf_tensor("mem", [P, WORDS], F32)), WORDS)
        psum = [ctx.enter_context(nc.psum_tensor(f"bank{i}", [P, 512], F32)) for i in range(8)]

        wqk = mem.take(KD * HP * NK).rearrange("p (k n) -> p k n", k=KD)
        identf = mem.take(P)
        identb = mem.take(P // 2, BF16)
        xs = mem.take(KD * P).rearrange("p (k t) -> p k t", k=KD)
        sim = mem.take(HP * NK)
        s16 = mem.take(HP * TOPK).rearrange("p (h c n) -> p h c n", h=FH, c=2)
        i16 = mem.take(HP * TOPK, I32).rearrange("p (h c n) -> p h c n", h=FH, c=2)
        i64 = mem.take(FH * TOPK, I32).rearrange("p (h n) -> p h n", h=FH)
        gate = mem.take(2)
        one = mem.take(1)
        k64 = mem.take(1, I32)
        left = [mem.take(NK) for _ in range(2)]
        cand, c1, wkey, ikey = (mem.take(FH * NC).rearrange("p (h n) -> p h n", h=FH) for _ in range(4))
        cidx = mem.take(FH * NC, I32).rearrange("p (h n) -> p h n", h=FH)
        pcode = mem.take(FH * NC, I32).rearrange("p (h n) -> p h n", h=FH)
        best = mem.take(FH * 16).rearrange("p (h n) -> p h n", h=FH)
        kA, kB = (mem.take(FH * TOPK).rearrange("p (h n) -> p h n", h=FH) for _ in range(2))
        wA, wB, eH, eL = (mem.take(P, I32) for _ in range(4))
        wf = mem.take(P)
        wres = mem.take(P)
        tok = mem.take(5 * P // 2, BF16).rearrange("p (c n) -> p c n", c=5)
        tokS = mem.take(5 * P // 2, BF16).rearrange("p (c t) -> p c t", c=5)
        iota = mem.take(P * TK // 2, BF16).rearrange("p (c t) -> p c t", c=P)
        mark = mem.at

        x_sb = [mem.take(TB * D).rearrange("p (t d) -> p t d", t=TB) for _ in range(3)]
        c_sb = [mem.take(TB * D).rearrange("p (t d) -> p t d", t=TB) for _ in range(2)]
        xn_sb = mem.take(TB * D).rearrange("p (t d) -> p t d", t=TB)
        xT = mem.take(KD * S).rearrange("p (k t) -> p k t", k=KD)
        cT = mem.take(KD * S).rearrange("p (k t) -> p k t", k=KD)
        proj = [mem.take(S) for _ in range(2)]
        rest = mem.take(S)
        part = [mem.take(3 * S // 2, BF16).rearrange("p (c t) -> p c t", c=3) for _ in range(2)]
        qst = [mem.take(HG * S // 2, BF16).rearrange("p (h t) -> p h t", h=HG) for _ in range(4)]
        kst = [mem.take(HG * S // 2, BF16).rearrange("p (h t) -> p h t", h=HG) for _ in range(4)]
        v_sb = [mem.take(TB * H * 32).rearrange("p (t h c) -> p t h c", t=TB, h=H) for _ in range(2)]
        p_sb = [mem.take(HG * S).rearrange("p (h t) -> p h t", h=HG) for _ in range(3)]
        oT = [mem.take(S) for _ in range(2)]
        attn = mem.take(TB * D).rearrange("p (t d) -> p t d", t=TB)
        aT = mem.take(KD * S).rearrange("p (k t) -> p k t", k=KD)
        x1 = [mem.take(CH * D).rearrange("p (t d) -> p t d", t=CH) for _ in range(2)]
        y_sb = [mem.take(CH * D).rearrange("p (t d) -> p t d", t=CH) for _ in range(2)]
        rest_own = y_sb[0].rearrange("p t d -> p (t d)")
        xnT = [mem.take(KD * TC).rearrange("p (k t) -> p k t", k=KD) for _ in range(2)]
        w_sb = [mem.take(KD * D).rearrange("p (k n) -> p k n", k=KD) for _ in range(4)]
        Wq_sb, Wk_sb, Wv_sb, Wo_sb = w_sb
        bqk = mem.take(2 * KD).rearrange("p (w k) -> p w k", w=2)
        nw = mem.take(KD)
        brow = mem.take(2 * D)
        ones = mem.take(P)
        nmx = [mem.take(TB * HG).rearrange("p (t h) -> p t h", t=TB) for _ in range(2)]
        mres = mem.take(TB * HG).rearrange("p (t h) -> p t h", t=TB)
        mpart = [mem.take(TB * MR * HG // 2, BF16).rearrange("p (t c h) -> p t c h", t=TB, c=MR) for _ in range(2)]
        mrow = [mem.take(S // 2, BF16) for _ in range(2)]
        rden = mem.take(TB * HG).rearrange("p (t h) -> p t h", t=TB)
        st6 = mem.take(TB * 6).rearrange("p (t c) -> p t c", t=TB)
        mv = mem.take(TB * 2).rearrange("p (t c) -> p t c", t=TB)
        rstd = [mem.take(TB) for _ in range(2)]
        half = mem.take(TB)
        st6e = mem.take(CH * 6).rearrange("p (t c) -> p t c", t=CH)
        mve = mem.take(CH * 2).rearrange("p (t c) -> p t c", t=CH)
        chain = [mem.take(CH) for _ in range(6)]
        dn_sb = [mem.take(2 * D).rearrange("p (j d) -> p j d", j=2) for _ in range(2)]
        dT = [mem.take(KD * 2 * P).rearrange("p (k j e) -> p k j e", k=KD, j=2) for _ in range(2)]
        wq_sb = [mem.take(KD * 2 * P).rearrange("p (k n) -> p k n", k=KD) for _ in range(2)]
        ky_sb = [mem.take(2 * P).rearrange("p (c d) -> p c d", c=2) for _ in range(2)]
        wqT = mem.take(2 * KD * P).rearrange("p (c k f) -> p c k f", c=2, k=KD)
        kyT = mem.take(2 * NK).rearrange("p (c n) -> p c n", c=2)

        mem.at = mark
        downT = mem.take(KD * JL * P).rearrange("p (k j e) -> p k j e", k=KD, j=JL)
        up_sb = mem.take(JL * D).rearrange("p (j d) -> p j d", j=JL)
        coef = [mem.take(JL * TC).rearrange("p (j t) -> p j t", j=JL) for _ in range(2)]
        xm = [mem.take(KD * TC).rearrange("p (k t) -> p k t", k=KD) for _ in range(2)]
        oh = [mem.take(P * TK // 2, BF16).rearrange("p (c t) -> p c t", c=P) for _ in range(2)]
        oj = [mem.take(JL * TK // 2, BF16).rearrange("p (c t) -> p c t", c=JL) for _ in range(2)]
        ow = [mem.take(3 * JL * TK // 2, BF16).rearrange("p (w c t) -> p w c t", w=3, c=JL) for _ in range(2)]
        gm = [mem.take(2 * TC).rearrange("p (j t) -> p j t", j=2) for _ in range(4)]
        tokT = [mem.take(5 * P // 2, BF16).rearrange("p (c t) -> p c t", c=5) for _ in range(4)]
        outT = mem.take(KD * TC).rearrange("p (k t) -> p k t", k=KD)
        xr = mem.take(CH * D).rearrange("p (t d) -> p t d", t=CH)

        SLOTS = NG + 5
        NA = 6
        TASKS = ([("search", h) for h in range(FH)] + [("candidates", 0)] + [("choose", s) for s in range(4)] +
                 [("keys", 0)] + [("extract", s) for s in range(4)])

        def spread(n_tiles, first, steps):
            n = n_tiles * len(TASKS)
            return [(first + t * (steps - first) // n, t // len(TASKS), *TASKS[t % len(TASKS)]) for t in range(n)]

        def choice_start(tile):
            return 2 * HG + 2 * tile

        choice = {}
        for _t in range(NA):
            for _s, _, _kind, _i in spread(1, 5, 32):
                choice.setdefault((choice_start(_t) + _s // 16, _s % 16), []).append((_t, _kind, _i))
        before = [(0, "xT", (0, 0)), (0, "xT", (0, 1)), (0, "cT", (0, 0)), (0, "cT", (0, 1)), (0, "proj", (0, 0)),
                  (0, "proj", (0, 1)), (0, "proj", (0, 2)), (0, "proj", (0, 3)), (0, "v", (0, 0)), (0, "v", (0, 1))]
        plan = []
        for g in range(SLOTS):
            b, r = g // HG, g % HG
            ev = []
            if 1 <= g <= NG:
                ev.append((3, "max", g - 1))
            if 3 <= g < NG + 3:
                ev.append((4, "oT", g - 3))
            if r == 0 and b + 1 < B:
                ev += [(11, "xT", (b + 1, 0)), (12, "xT", (b + 1, 1)), (13, "cT", (b + 1, 0)), (14, "cT", (b + 1, 1))]
            if r == 1 and b + 1 < B:
                ev += [(2 + 3 * n, "proj", (b + 1, n)) for n in range(4)]
            if r == 2 and b + 1 < B:
                ev += [(3, "v", (b + 1, 0)), (5, "v", (b + 1, 1))]
            if r == 2 and b >= 1:
                ev += [(8, "aT", (b - 1, 0)), (9, "aT", (b - 1, 1)), (12, "o", (b - 1, 0)), (14, "o", (b - 1, 1))]
            if r == 3 and b >= 1:
                ev += [(6, "yT", (b - 1, 0)), (8, "yT", (b - 1, 1))]
            if g % 2 == 0 and g >= choice_start(0):
                tile = (g - choice_start(0)) // 2
                if tile < NA:
                    ev += [(1, "sim", (tile, 0)), (2, "sim", (tile, 1))]
                if 1 <= tile <= NA:
                    ev.append((6, "tok", tile - 1))
            if g < JL // 2:
                ev.append((7, "down", g))
            if g < HP // 2:
                ev += [(9, "wqT", g), (10, "kyT", g), (15, "wqk", g)]
            plan.append(sorted(ev, key=lambda e: e[0]))
        order = {(n, i): e for e, (_, n, i) in enumerate(before + [e for s in plan for e in s])}

        misc_full = [sem("misc_full0"), sem("misc_full1")]
        misc_read = [sem("misc_read0"), sem("misc_read1")]

        def place(name, index):
            e = order[(name, index)]
            return e % 2, e // 2, psum[6 + e % 2]

        def wait_taken(eng, name, index):
            bank, n, _ = place(name, index)
            eng.wait_ge(misc_read[bank], n + 1)

        def wait_filled(eng, name, index):
            bank, n, ps = place(name, index)
            eng.wait_ge(misc_full[bank], n + 1)
            return ps, misc_read[bank]

        consts = sem("consts")
        w_ld = sem("w_ld")
        x_ld = [sem(f"x_ld{i}") for i in range(3)]
        c_ld = [sem(f"c_ld{i}") for i in range(2)]
        ln_stat = sem("ln_stat")
        ln_rstd = sem("ln_rstd")
        ln_out = sem("ln_out")
        split = sem("split")
        split_own = sem("split_own")
        part_wr = [sem(f"part_wr{i}") for i in range(4)]
        st_ld = [sem(f"st_ld{i}") for i in range(4)]
        mr_wr = [sem(f"mr_wr{i}") for i in range(2)]
        mr_ld = [sem(f"mr_ld{i}") for i in range(4)]
        s_full = sem("s_full")
        s_max = sem("s_max")
        mp_done = sem("mp_done")
        t_full = sem("t_full")
        p_ready = sem("p_ready")
        pv_done = sem("pv_done")
        o_ev = sem("o_ev")
        nrm = sem("nrm")
        e_stat = sem("e_stat")
        e_scale = sem("e_scale")
        e_fin = sem("e_fin")
        e_out = sem("e_out")
        x1_wr = [sem(f"x1_wr{i}") for i in range(2)]
        xn_wr = [sem(f"xn_wr{i}") for i in range(2)]
        dT_wr = [sem(f"dT_wr{i}") for i in range(2)]
        dn_ld = [sem(f"dn_ld{i}") for i in range(2)]
        wq_ld = [sem(f"wq_ld{i}") for i in range(2)]
        phase = sem("phase")

        HBN = 8

        dt_ld = [sem(f"dt_ld{i}") for i in range(4)]
        up_ld = [sem(f"up_ld{i}") for i in range(4)]
        econst = sem("econst")
        iconst = sem("iconst")
        pcd = sem("pcd")
        xs_ld = sem("xs_ld")
        xm_ld = [sem(f"xm_ld{i}") for i in range(2)]
        xr_ld = sem("xr_ld")
        sim_mm = sem("sim_mm")
        sim_ev = sem("sim_ev")
        dve_step = sem("dve_step")
        pool_step = sem("pool_step")
        st1 = sem("st1")
        cix = sem("cix")
        key = sem("key")
        dec_w = sem("dec_w")
        dec = sem("dec")
        wsp = sem("wsp")
        tok_mm = sem("tok_mm")
        tok_ev = sem("tok_ev")
        tok_wr = sem("tok_wr")
        tokT_ld = [sem(f"tokT_ld{i}") for i in range(4)]
        oh_rdy = sem("oh_rdy")
        ow_rdy = sem("ow_rdy")
        ow_own = sem("ow_own")
        c_mm = sem("c_mm")
        c_ev = sem("c_ev")
        g_mm = sem("g_mm")
        g_act = sem("g_act")
        m_rdy = sem("m_rdy")
        o_mm = sem("o_mm")
        ot_ev = sem("ot_ev")
        fin_mm = sem("fin_mm")
        fin_add = sem("fin_add")
        out_wr = sem("out_wr")

        def pool_splits(b, n):
            return n // 2 if b == 0 else 4 * b + n - 2

        def parts_ready(eng, b, n):
            if b == 0 and n % 2:
                eng.wait_ge(split_own, 4 * (n // 2 + 1))
            else:
                eng.wait_ge(split, 4 * (pool_splits(b, n) + 1))

        def sim_filled(eng, tile):
            if isinstance(tile, int) and tile < NA:
                if tile >= 0:
                    wait_filled(eng, "sim", (tile, 1))
            else:
                eng.wait_ge(sim_mm, tile * 2 - (2 * NA - 2))

        def sim_taken(eng, tile):
            if isinstance(tile, int) and tile < NA:
                wait_taken(eng, "sim", (tile, 0))
                wait_taken(eng, "sim", (tile, 1))
            else:
                eng.wait_ge(sim_ev, tile * 2 - (2 * NA - 2))

        def tok_filled(eng, tile):
            if isinstance(tile, int) and tile < NA:
                if tile >= 0:
                    wait_filled(eng, "tok", tile)
            else:
                eng.wait_ge(tok_mm, tile - (NA - 1))

        OWN = [q for q in range(16) if q % 3 != 0]

        def block_weighed(eng, c):
            if isinstance(c, int) and c in OWN:
                eng.wait_ge(ow_own, OWN.index(c) + 1)
            elif isinstance(c, int) and c < 16:
                if c >= 0:
                    eng.wait_ge(ow_rdy, c + 1 - sum(o < c for o in OWN))
            else:
                eng.wait_ge(ow_rdy, c + (1 - len(OWN)))

        def at_least(eng, s, value):
            if isinstance(value, int) and value <= 0:
                return
            eng.wait_ge(s, value)

        class Steps:

            def __init__(self, eng, s):
                self.eng, self.s, self.n = eng, s, 0

            def count(self, instruction):
                instruction.then_inc(self.s, 1)
                self.n += 1
                return self.n

            def after(self, n):
                self.eng.wait_ge(self.s, n)

            def all(self):
                if self.n:
                    self.after(self.n)

            def restart(self):
                if self.n:
                    self.after(self.n)
                    self.eng.sem_clear(self.s)
                    self.n = 0

        def runs(eng, run):
            run(-1, 3, NA, 4, -1)
            with eng.Fori(0, 2) as i:
                run(i * 2 + 2, 2, i * 3 + (NA + 4), 3, None)
            run(6, 1, TILES, 0, 6)
            run(7, 1, TILES, 0, 7)
            run(8, 1, TILES, 0, 8)

        def on(k, lo, hi):
            return k is None or lo <= k <= hi

        FEW = 5

        def walk(k0, n_slots, t0, n_tiles, kk0):
            tasks = spread(n_tiles, 0, 16 * n_slots)
            if kk0 == -1:
                tasks = [(16 * n // FEW if n < FEW else 16 + 32 * (n - FEW) // (len(tasks) - FEW), *tasks[n][1:])
                         for n in range(len(tasks))]
            turned = t0 - 2 if kk0 in (None, 6) else t0 - 1
            for x in range(16 * n_slots):
                sl = x // 16
                kk = None if kk0 is None else kk0 + sl
                par = (0 if kk0 is None else kk0) + sl
                now = {"tasks": [(t0 + t, kind, i) for s, t, kind, i in tasks if s == x],
                       "fetch": [t0 + (t + 1) for s, t, kind, i in tasks if s == x and (kind, i) == ("search", 4)],
                       "mult": [(t0 + (t + 1), x - s) for s, t, kind, i in tasks
                                if x - s in (0, 1) and (kind, i) == ("choose", 3)],
                       "turn": [t0 + t for s, t, kind, i in tasks if s + 3 == x and (kind, i) == ("extract", 3)]}
                if x == 2 and kk0 in (None, 6):
                    now["turn"].insert(0, t0 - 1)
                if now["turn"]:
                    turned = now["turn"][-1]
                now["turned"] = turned
                yield x % 16, k0 + sl, par % 2, kk, now

        def back(k, par, kk, q, lag):
            q -= lag
            if q >= 0:
                return k, par, kk, q
            return k - 1, 1 - par, None if kk is None else kk - 1, q + 16

        block = ctx.enter_context(nc.Block())

        @block.sync
        def _(sp):
            for w, src in zip(w_sb, (Wq, Wk, Wv, Wo)):
                sp.dma_start(w, src.rearrange("(k p) n -> p k n", p=P)).then_inc(w_ld, 16)
            for n, src in enumerate((bq, bk)):
                for k in range(KD):
                    sp.dma_start(bqk[:, n, k:k + 1], src[k * P:(k + 1) * P].rearrange("(p o) -> p o", o=1)).then_inc(w_ld, 16)
            for k in range(KD):
                sp.dma_start(nw[:, k:k + 1], norm_w[k * P:(k + 1) * P].rearrange("(p o) -> p o", o=1)).then_inc(w_ld, 16)
            for n, src in enumerate((bv, bo)):
                sp.dma_start(brow[0:1, n * D:(n + 1) * D], src.rearrange("(o n) -> o n", o=1)).then_inc(w_ld, 16)

            def load_x(b):
                if b >= 3:
                    wait_taken(sp, "o", (b - 3, 1))
                sp.dma_start(x_sb[b % 3], x[b].rearrange("(t p) d -> p t d", p=P)).then_inc(x_ld[b % 3], 16)
                if b >= 2:
                    wait_taken(sp, "cT", (b - 2, 1))
                sp.dma_start(c_sb[b % 2], ctx_in[b].rearrange("(t p) d -> p t d", p=P)).then_inc(c_ld[b % 2], 16)

            def store_parts(b, n):
                parts_ready(sp, b, n)
                dst = parts_d[b, n % 2, :, (n // 2) * P:(n // 2 + 1) * P, :].rearrange("c p t -> p c t")
                sp.dma_start(dst, part[n % 2]).then_inc(part_wr[n], 16)

            def load_stacks(g):
                b, r = g // HG, g % HG
                for n in (2 * (r // 2), 2 * (r // 2) + 1):
                    sp.wait_ge(part_wr[n], 16 * (b + 1))
                if g >= 4:
                    sp.wait_ge(pv_done, 4 * (g - 3))
                for w, (dst, pick) in enumerate(((qst, QPART), (kst, KPART))):
                    for s, c in enumerate(pick):
                        src = parts_d[b, w, c, r * HG * DK:(r + 1) * HG * DK, :].rearrange("(h d) t -> d h t", d=DK)
                        sp.dma_start(dst[g % 4][s * DK:(s + 1) * DK], src).then_inc(st_ld[g % 4], 16)

            def relay_max(g):
                wait_taken(sp, "max", g)
                sp.dma_start(mrow_d[g], mrow[g % 2][0:MR * HG, :]).then_inc(mr_wr[g % 2], 16)
                sp.wait_ge(mr_wr[g % 2], 16 * (g // 2 + 1))
                sp.dma_start(qst[g % 4][SK:SK + MR], mrow_d[g].rearrange("(c h) t -> c h t", c=MR)).then_inc(mr_ld[g % 4], 16)

            def load_setup(n):
                if n < JL // 2:
                    if n >= 2:
                        wait_taken(sp, "down", n - 2)
                    src = down.rearrange("(p j) d -> p j d", j=JL)
                    sp.dma_start(dn_sb[n % 2], src[:, 2 * n:2 * n + 2, :]).then_inc(dn_ld[n % 2], 16)
                if n < HP // 2:
                    if n >= 2:
                        wait_taken(sp, "kyT", n - 2)
                    sp.dma_start(wq_sb[n % 2], wq.rearrange("(k p) n -> p k n", p=P)[:, :, n * 2 * P:(n + 1) * 2 * P])\
                      .then_inc(wq_ld[n % 2], 16)
                    sp.dma_start(ky_sb[n % 2][0:NK], keys[n]).then_inc(wq_ld[n % 2], 16)

            def store_half(b, e):
                n = 2 * b + e
                rows = slice(b * S + e * TC, b * S + (e + 1) * TC)
                sp.wait_ge(e_out, 2 * (n + 1))
                sp.dma_start(x1_d[rows, :].rearrange("(t p) d -> p t d", p=P), x1[e]).then_inc(x1_wr[e], 16)
                wait_taken(sp, "yT", (b, e))
                sp.dma_start(xn_d[:, :, rows], xnT[e]).then_inc(xn_wr[e], 16)
                if n == HBN - 1:
                    sp.dma_start(xn_d[:, :, NT:NT + P], xnT[e][:, :, TC - P:TC]).then_inc(xn_wr[e], 16)

            def load_sim_input(tile):
                if not isinstance(tile, int) or tile > 0:
                    sim_filled(sp, tile - 1)
                sp.dma_start(xs, xn_d[:, :, bass.ds(tile * P, P)]).then_inc(xs_ld, 16)

            def store_choice(tile):
                if isinstance(tile, int) and tile < NA:
                    wait_taken(sp, "tok", tile)
                else:
                    sp.wait_ge(tok_ev, tile - (NA - 1))
                sp.dma_start(tok_d[bass.ds(tile * P, P), :], tokS.rearrange("p c t -> p (c t)")).then_inc(tok_wr, 16)

            load_x(0)
            load_x(1)
            load_setup(0)
            load_setup(1)
            for n in range(4):
                store_parts(0, n)
            load_stacks(0)
            for g in range(SLOTS):
                b, r = g // HG, g % HG
                if 1 <= g <= NG:
                    relay_max(g - 1)
                if g + 1 < NG:
                    load_stacks(g + 1)
                if r == 3 and b + 2 < B:
                    load_x(b + 2)
                load_setup(g + 2)
                if r == 1 and b + 1 < B:
                    for n in range(4):
                        store_parts(b + 1, n)
                if r == 3 and b >= 1:
                    store_half(b - 1, 0)
                    store_half(b - 1, 1)
                if g < JL // 2:
                    wait_taken(sp, "down", g)
                    sp.dma_start(downT_d[:, :, 2 * g:2 * g + 2, :], dT[g % 2]).then_inc(dT_wr[g % 2], 16)
                tile = (g + 1 - choice_start(0)) // 2
                if g == choice_start(tile) - 1 and 0 <= tile < NA:
                    for e in range(2):
                        sp.wait_ge(xn_wr[e], 16 * (tile // TB + 1))
                    load_sim_input(tile)
                if g == choice_start(tile) and 1 <= tile <= NA:
                    store_choice(tile - 1)
            for s in (*x1_wr, xn_wr[0]):
                sp.wait_ge(s, 16 * B)
            sp.wait_ge(xn_wr[1], 16 * (B + 1))
            for s in dT_wr:
                sp.wait_ge(s, 16 * (JL // 4))
            sp.wait_ge(tok_wr, 16 * NA)
            sp.sem_inc(phase, 1)
            sp.wait_ge(phase, 5)

            def load_choice(tile, r):
                if isinstance(tile, int):
                    block_weighed(sp, (tile - 3) * BPT - 1)
                    block_weighed(sp, (tile - 3) * BPT - 2)
                sp.wait_ge(tok_wr, (tile + 1) * 16)
                sp.dma_start(tokT[r].rearrange("p c t -> p (c t)"), tok_d[bass.ds(tile * P, P), :]).then_inc(tokT_ld[r], 16)

            load_choice(0, 0)
            load_sim_input(NA)
            load_choice(1, 1)
            JQ = JL // 4
            for i in range(4):
                sp.dma_start(downT[:, :, i * JQ:(i + 1) * JQ, :], downT_d[:, :, i * JQ:(i + 1) * JQ, :]).then_inc(dt_ld[i], 16)
            for i in range(4):
                src = up.rearrange("(p j) d -> p j d", j=JL)[:, i * JQ:(i + 1) * JQ, :]
                sp.dma_start(up_sb[:, i * JQ:(i + 1) * JQ, :], src).then_inc(up_ld[i], 16)

            def run(*where):
                for q, k, par, kk, now in walk(*where):
                    if q == 0 and on(kk, 1, 8):
                        at_least(sp, out_wr, (k - 1) * 16)
                        sp.dma_start(xr, x1_d[bass.ds((k - 1) * TC, TC), :].rearrange("(t p) d -> p t d", p=P))\
                          .then_inc(xr_ld, 16)
                    if q == 2 and on(kk, -1, 6):
                        at_least(sp, g_mm, k * 16)
                        sp.dma_start(xm[1 - par], xn_d[:, :, bass.ds((k + 1) * TC, TC)]).then_inc(xm_ld[1 - par], 16)
                    for tile in now["turn"]:
                        store_choice(tile)
                    for tile in now["fetch"]:
                        load_sim_input(tile)
                    if q == 6 and on(kk, 1, 8):
                        sp.wait_ge(fin_add, k)
                        dst = out.rearrange("b s d -> (b s) d")[bass.ds((k - 1) * TC, TC), :]
                        sp.dma_start(dst.rearrange("(t p) d -> p t d", p=P), xr).then_inc(out_wr, 16)
                    if q == 6 and on(kk, 0, 6):
                        load_choice(k * 2 + 3, 3 if par == 0 else 1)
                    if q == 15 and on(kk, -1, 5):
                        load_choice(k * 2 + 4, 0 if par == 0 else 2)

            runs(sp, run)
            sp.wait_ge(out_wr, 8 * 16)

        @block.gpsimd
        def _(pool):
            nc.gpsimd.memset(identf, 0.0).then_inc(consts, 1)
            nc.gpsimd.memset(ones, 1.0).then_inc(consts, 1)
            nc.gpsimd.memset(half, -0.5).then_inc(consts, 1)
            nc.gpsimd.memset(k64, NK).then_inc(econst, 1)
            nc.gpsimd.memset(gate, 0.0).then_inc(econst, 1)
            nc.gpsimd.memset(one, 1.0).then_inc(econst, 1)
            nc.gpsimd.iota(pcode, pattern=[[0, FH], [1, NC]], base=8, channel_multiplier=0).then_inc(econst, 1)
            pool.wait_ge(consts, 3)
            nc.gpsimd.affine_select(out=identf, in_=identf, compare_op=ALU.not_equal, fill=1.0, base=0,
                                    pattern=[[-1, P]], channel_multiplier=1).then_inc(consts, 1)
            pool.wait_ge(consts, 4)
            nc.gpsimd.tensor_copy(identb, identf).then_inc(consts, 1)
            for i in range(4):
                pool.wait_ge(consts, 5 + i)
                nc.gpsimd.memset(kst[i][SK:SK + MR], 1.0).then_inc(consts, 1)
            pool.wait_ge(consts, 9)
            for i in range(2):
                nc.gpsimd.memset(v_sb[i], 1.0).then_inc(consts, 1)

            steps = Steps(pool, pool_step)

            def candidate_numbers(u):
                at_least(pool, st1, (u + 1) * FH)
                at_least(pool, key, u)
                if isinstance(u, int) and u == 0:
                    pool.wait_ge(pcd, 1)
                steps.all()
                ii = i16
                n0 = steps.count(nc.gpsimd.tensor_tensor(i64, ii[:, :, 0, :], k64.unsqueeze(2).to_broadcast([P, FH, TOPK]),
                                                         ALU.mult))
                steps.after(n0)
                for a, rows, n, at in SEGS:
                    o = cidx[:, :, at:at + rows * n].rearrange("p h (a b) -> p h a b", a=rows)
                    i0 = i64[:, :, a:a + rows].unsqueeze(3).to_broadcast([P, FH, rows, n])
                    i1 = ii[:, :, 1, 0:n].unsqueeze(2).to_broadcast([P, FH, rows, n])
                    if rows == 1:
                        o, i0, i1 = o[:, :, 0, :], i0[:, :, 0, :], i1[:, :, 0, :]
                    steps.count(nc.gpsimd.tensor_tensor(o, i0, i1, ALU.add))
                steps.all()
                nc.gpsimd.tensor_tensor(cidx, cidx, pcode, ALU.add).then_inc(cix, 1)

            def weight_parts(v):
                w, c = wf, tok
                pool.wait_ge(dec_w, v + 1)
                tok_filled(pool, v - 1)
                steps.all()
                n = steps.count(nc.gpsimd.tensor_tensor(c[:, 2, :], w, one.to_broadcast([P, P]), ALU.mult))
                steps.after(n)
                n = steps.count(nc.gpsimd.tensor_tensor(wres, w, c[:, 2, :], ALU.subtract))
                steps.after(n)
                n = steps.count(nc.gpsimd.tensor_copy(c[:, 3, :], wres))
                steps.after(n)
                nc.gpsimd.tensor_tensor(c[:, 4, :], wres, c[:, 3, :], ALU.subtract).then_inc(wsp, 1)

            def first_rstd(b):
                pool.wait_ge(ln_stat, 8 * (b + 1))
                nc.gpsimd.tensor_scalar(rstd[0], mv[:, :, 1], EPS, None, ALU.add).then_inc(ln_rstd, 1)
                pool.wait_ge(ln_rstd, 2 * b + 1)
                nc.gpsimd.tensor_tensor(rstd[1], rstd[0], half, ALU.pow).then_inc(ln_rstd, 1)

            def split_projection(b, n):
                e = pool_splits(b, n)
                f, c = proj[n % 2], part[n % 2]
                wait_taken(pool, "proj", (b, n))
                if b or n >= 2:
                    pool.wait_ge(part_wr[(n + 2) % 4], 16 * (b if n < 2 else b + 1))
                nc.gpsimd.tensor_copy(c[:, 0, :], f).then_inc(split, 1)
                pool.wait_ge(split, 4 * e + 1)
                nc.gpsimd.tensor_tensor(rest, f, c[:, 0, :], ALU.subtract).then_inc(split, 1)
                pool.wait_ge(split, 4 * e + 2)
                nc.gpsimd.tensor_copy(c[:, 1, :], rest).then_inc(split, 1)
                pool.wait_ge(split, 4 * e + 3)
                nc.gpsimd.tensor_tensor(c[:, 2, :], rest, c[:, 1, :], ALU.subtract).then_inc(split, 1)

            def second_scale(n):
                a, r, v1, v2, v3, s2 = chain
                base = 6 * n
                pool.wait_ge(e_stat, 4 * (n + 1))
                if n:
                    pool.wait_ge(e_out, 2 * n)
                nc.gpsimd.tensor_scalar(a, mve[:, :, 1], EPS, None, ALU.add).then_inc(e_scale, 1)
                pool.wait_ge(e_scale, base + 1)
                nc.gpsimd.tensor_tensor(r, a, half[:, 0:CH], ALU.pow).then_inc(e_scale, 1)
                pool.wait_ge(e_scale, base + 2)
                nc.gpsimd.tensor_tensor(v1, mve[:, :, 1], r, ALU.mult).then_inc(e_scale, 1)
                pool.wait_ge(e_scale, base + 3)
                nc.gpsimd.tensor_tensor(v2, v1, r, ALU.mult).then_inc(e_scale, 1)
                pool.wait_ge(e_scale, base + 4)
                nc.gpsimd.tensor_scalar(v3, v2, EPS, None, ALU.add).then_inc(e_scale, 1)
                pool.wait_ge(e_scale, base + 5)
                nc.gpsimd.tensor_tensor(v2, v3, half[:, 0:CH], ALU.pow).then_inc(e_scale, 1)
                pool.wait_ge(e_scale, base + 6)
                nc.gpsimd.tensor_tensor(s2, v2, r, ALU.mult).then_inc(e_fin, 1)

            first_rstd(0)
            for n in (0, 2):
                split_projection(0, n)
            numbers = p_sb[2].rearrange("p h t -> p (h t)").bitcast(I32).rearrange("p (c t) -> p c t", c=P)
            nc.gpsimd.iota(numbers, pattern=[[1, P], [0, TK]], base=0, channel_multiplier=0).then_inc(iconst, 1)
            pool.wait_ge(iconst, 1)
            nc.gpsimd.tensor_copy(iota, numbers).then_inc(iconst, 1)
            for g in range(SLOTS):
                b, r = g // HG, g % HG
                tile = (g - choice_start(0)) // 2
                ends = g == choice_start(tile) + 1 and 0 <= tile < NA
                if r == 0 and b + 1 < B:
                    first_rstd(b + 1)
                if ends:
                    steps.restart()
                    candidate_numbers(tile)
                if r == 1 and b + 1 < B:
                    for n in range(4):
                        split_projection(b + 1, n)
                if r == 2 and b >= 1:
                    second_scale(2 * (b - 1))
                    second_scale(2 * (b - 1) + 1)
                if ends:
                    weight_parts(tile)
            pool.wait_ge(e_fin, 2 * B)
            pool.sem_inc(phase, 1)
            pool.wait_ge(phase, 5)

            def weigh(c, par, q):
                pool.wait_ge(oh_rdy, c * 2 + 2)
                at_least(pool, c_mm, c - 1)
                i0 = oj[q % 2].unsqueeze(1).to_broadcast([P, 3, JL, TK])
                t0 = q % BPT * TK
                i1 = tokT[2 * (1 - par) + q // BPT][:, 2:5, t0:t0 + TK].unsqueeze(2).to_broadcast([P, 3, JL, TK])
                nc.gpsimd.tensor_tensor(ow[q % 2], i0, i1, ALU.mult).then_inc(ow_rdy, 1)

            def run(*where):
                for q, k, par, kk, now in walk(*where):
                    for tile, kind, i in now["tasks"]:
                        if kind == "candidates":
                            candidate_numbers(tile)
                    if on(kk, -1, 6) and not (kk == -1 and q in OWN):
                        weigh((k + 1) * 16 + q, par, q)
                    for tile, kind, i in now["tasks"]:
                        if (kind, i) == ("extract", 3):
                            weight_parts(tile)
                steps.restart()

            steps.restart()
            runs(pool, run)

        @block.scalar
        def _(act):
            act.wait_ge(w_ld, 12 * 16)

            def take(name, index):
                if name in ("o", "oT"):
                    return
                ps, done = wait_filled(act, name, index)
                if name in ("xT", "cT"):
                    b, e = index
                    dst = xT if name == "xT" else cT
                    src = ps[:, :].rearrange("p (k t) -> p k t", k=KD)
                    nc.scalar.copy(dst[:, :, e * TC:(e + 1) * TC], src).then_inc(done, 1)
                elif name == "proj":
                    b, n = index
                    if b or n >= 2:
                        parts_ready(act, *((b, n - 2) if n >= 2 else (b - 1, n + 2)))
                    nc.scalar.activation(proj[n % 2], ps[:, :], ACT.Identity, bias=bqk[:, n % 2, n // 2:n // 2 + 1])\
                      .then_inc(done, 1)
                elif name == "v":
                    b, e = index
                    if b >= 2:
                        act.wait_ge(pv_done, 16 * (b - 1))
                    if b < 2 and e == 0:
                        act.wait_ge(consts, 11)
                    src = ps[:, :].rearrange("p (t h c) -> p t h c", t=CH, h=H)
                    for t in range(CH):
                        i = nc.scalar.copy(v_sb[b % 2][:, e * CH + t, :, 0:DK], src[:, t])
                    i.then_inc(done, 1)
                elif name == "max":
                    if index >= 2:
                        act.wait_ge(mr_wr[index % 2], 16 * (index // 2))
                    nc.scalar.copy(mrow[index % 2][0:MR * HG, :], ps[0:MR * HG, 0:S // 2].bitcast(BF16)).then_inc(done, 1)
                elif name == "aT":
                    b, e = index
                    src = ps[:, :].rearrange("p (k t) -> p k t", k=KD)
                    nc.scalar.copy(aT[:, :, e * TC:(e + 1) * TC], src).then_inc(done, 1)
                elif name == "yT":
                    b, e = index
                    if b >= 1:
                        act.wait_ge(xn_wr[e], 16 * b)
                    src = ps[:, :].rearrange("p (k t) -> p k t", k=KD)
                    for c in range(KD):
                        i = nc.scalar.activation(xnT[e][:, c, :], src[:, c, :], ACT.Copy, scale=nw[:, c:c + 1])
                    i.then_inc(done, 1)
                elif name == "down":
                    src = ps[:, :].rearrange("p (k j e) -> p k j e", k=KD, j=2)
                    if index >= 2:
                        act.wait_ge(dT_wr[index % 2], 16 * (index // 2))
                    nc.scalar.copy(dT[index % 2], src).then_inc(done, 1)
                elif name == "sim":
                    tile, n = index
                    if tile and n == 0:
                        act.wait_ge(st1, FH * tile)
                    nc.scalar.copy(sim[:, n * 512:(n + 1) * 512], ps[:, :]).then_inc(done, 1)
                elif name == "tok":
                    if index:
                        act.wait_ge(tok_wr, 16 * index)
                    nc.scalar.copy(tokS, ps[:, 0:5 * P // 2].bitcast(BF16).rearrange("p (c t) -> p c t", c=5))\
                      .then_inc(done, 1)
                elif name == "wqT":
                    if index >= 1:
                        wait_taken(act, "wqk", index - 1)
                    nc.scalar.copy(wqT, ps[:, :].rearrange("p (c k f) -> p c k f", c=2, k=KD)).then_inc(done, 1)
                elif name == "kyT":
                    nc.scalar.copy(kyT, ps[:, 0:2 * NK].rearrange("p (c n) -> p c n", c=2)).then_inc(done, 1)
                elif name == "wqk":
                    src = ps[:, 0:KD * 2 * NK].rearrange("p (k n) -> p k n", k=KD)
                    nc.scalar.copy(wqk[:, :, index * 2 * NK:(index + 1) * 2 * NK], src).then_inc(done, 1)
                else:
                    raise ValueError(name)

            def probabilities(g, i):
                n = 16 * g + i
                quad, hh = 4 * g + i // HG, i % HG
                act.wait_ge(t_full, n + 1)
                if quad >= 3 and hh == 0:
                    act.wait_ge(pv_done, quad - 2)
                if quad == 2 and hh == 0:
                    act.wait_ge(iconst, 2)
                nc.scalar.activation(p_sb[quad % 3][:, hh, :], psum[3 + n % 2][:, :], ACT.Exp, scale=DK ** -0.5)\
                  .then_inc(p_ready, 1)

            for _, name, index in before:
                take(name, index)
            for g in range(SLOTS):
                for i in range(16):
                    if 2 <= g < NG + 2:
                        probabilities(g - 2, i)
                    if i == 2 and 3 <= g < NG + 3:
                        act.wait_ge(pv_done, 4 * (g - 2))
                        if g >= 5:
                            bank, n, _ = place("oT", g - 5)
                            act.wait_ge(misc_full[bank], n + 1)
                        nc.scalar.copy(oT[(g - 3) % 2], psum[5][:, :]).then_inc(o_ev, 1)
                    for _, name, index in [e for e in plan[g] if e[0] == i]:
                        take(name, index)
            wait_taken(act, "yT", (B - 1, 1))
            act.sem_inc(phase, 1)
            act.wait_ge(phase, 5)

            def take_sim(tile, n):
                act.wait_ge(sim_mm, tile * 2 - (2 * NA - 1 - n))
                if n == 0:
                    at_least(act, st1, tile * FH)
                nc.scalar.copy(sim[:, n * 512:(n + 1) * 512], psum[0][:, :]).then_inc(sim_ev, 1)

            def take_tok(tile):
                tok_filled(act, tile)
                act.wait_ge(tok_wr, tile * 16)
                nc.scalar.copy(tokS, psum[1][:, 0:5 * P // 2].bitcast(BF16).rearrange("p (c t) -> p c t", c=5))\
                  .then_inc(tok_ev, 1)

            def gelu(g, q):
                act.wait_ge(g_mm, g + 1)
                at_least(act, o_mm, g - 3)
                nc.scalar.activation(gm[q % 4], psum[4 + q % 2][:, :].rearrange("p (j t) -> p j t", j=2), ACT.Gelu)\
                  .then_inc(g_act, 1)

            def take_coef(k, par, q):
                act.wait_ge(c_mm, (k + 1) * 16 + (q + 1))
                if q == 0:
                    at_least(act, m_rdy, k * 16)
                src = psum[2 + q % 2][:, :].rearrange("p (t j) -> p j t", j=JL)
                nc.scalar.copy(coef[1 - par][:, :, q * TK:(q + 1) * TK], src).then_inc(c_ev, 1)

            def take_out(k):
                act.wait_ge(o_mm, k * 16)
                for c in range(KD):
                    i = nc.scalar.copy(outT[:, c, :], psum[6 + c][:, 0:TC])
                i.then_inc(ot_ev, 1)

            take_sim(NA, 0)
            take_sim(NA, 1)

            def run(*where):
                for q, k, par, kk, now in walk(*where):
                    if on(kk, 0, 7):
                        gelu(k * 16 + q, q)
                    k1, p1, kk1, q1 = back(k, par, kk, q, 1)
                    if on(kk1, -1, 6):
                        take_coef(k1, p1, q1)
                    if q == 2 and on(kk, 1, 8):
                        take_out(k)
                    for tile in now["turn"]:
                        take_tok(tile)
                    for tile, n in now["mult"]:
                        take_sim(tile, n)

            runs(act, run)

        @block.vector
        def _(dve):
            def first_norm(b):
                xb = x_sb[b % 3]
                dve.wait_ge(x_ld[b % 3], 16 * (b // 3 + 1))
                for t in range(TB):
                    nc.vector.bn_stats(st6[:, t, :], xb[:, t, :]).then_inc(ln_stat, 1)
                if b:
                    dve.wait_ge(ln_rstd, 2 * b)
                for t in range(TB):
                    dve.wait_ge(ln_stat, 8 * b + t + 1)
                    nc.vector.bn_aggr(mv[:, t, :], st6[:, t, :]).then_inc(ln_stat, 1)

            def first_norm_apply(b):
                dve.wait_ge(ln_rstd, 2 * (b + 1))
                dve.wait_ge(ln_stat, 8 * (b + 1))
                if b:
                    wait_filled(dve, "xT", (b - 1, 1))
                for t in range(TB):
                    nc.vector.tensor_scalar(xn_sb[:, t, :], x_sb[b % 3][:, t, :], mv[:, t, 0:1], rstd[1][:, t:t + 1],
                                            ALU.subtract, ALU.mult).then_inc(ln_out, 1)

            def max_parts(g):
                m, n = mpart[g % 2], nmx[g % 2]
                dve.wait_ge(s_max, 16 * (g + 1))
                if g >= 2:
                    wait_filled(dve, "max", g - 2)
                nc.vector.tensor_copy(m[:, :, 0, :], n).then_inc(mp_done, 1)
                dve.wait_ge(mp_done, 3 * g + 1)
                nc.vector.tensor_tensor(mres, n, m[:, :, 0, :], ALU.subtract).then_inc(mp_done, 1)
                dve.wait_ge(mp_done, 3 * g + 2)
                nc.vector.tensor_copy(m[:, :, 1, :], mres).then_inc(mp_done, 1)

            def normalise(g):
                ps, done = wait_filled(dve, "oT", g)
                if g >= 4 and g % 4 == 0:
                    wait_filled(dve, "aT", (g // 4 - 1, 1))
                v = ps[:, :].rearrange("p (t h c) -> p t h c", t=TB, h=HG)
                if g:
                    wait_taken(dve, "oT", g - 1)
                nc.vector.reciprocal(rden, v[:, :, :, DK]).then_inc(nrm, 1)
                dve.wait_ge(nrm, g + 1)
                r = g % HG
                o = attn[:, :, r * HG * DK:(r + 1) * HG * DK].rearrange("p t (h c) -> p t h c", h=HG)
                nc.vector.tensor_tensor(o, v[:, :, :, 0:DK], rden.unsqueeze(3).to_broadcast([P, TB, HG, DK]), ALU.mult)\
                  .then_inc(done, 1)

            def residual(b, e):
                n = 2 * b + e
                ps, done = wait_filled(dve, "o", (b, e))
                if b:
                    dve.wait_ge(x1_wr[e], 16 * b)
                nc.vector.tensor_tensor(x1[e], ps[:, :].rearrange("p (t d) -> p t d", t=CH),
                                        x_sb[b % 3][:, e * CH:(e + 1) * CH, :], ALU.add).then_inc(done, 1)
                wait_taken(dve, "o", (b, e))
                for t in range(CH):
                    nc.vector.bn_stats(st6e[:, t, :], x1[e][:, t, :]).then_inc(e_stat, 1)
                if n:
                    dve.wait_ge(e_fin, n)
                for t in range(CH):
                    dve.wait_ge(e_stat, 4 * n + t + 1)
                    nc.vector.bn_aggr(mve[:, t, :], st6e[:, t, :]).then_inc(e_stat, 1)

            def second_norm(b, e):
                n = 2 * b + e
                if n == 0:
                    dve.wait_ge(split_own, 8)
                dve.wait_ge(e_fin, n + 1)
                dve.wait_ge(e_stat, 4 * (n + 1))
                if b:
                    wait_filled(dve, "yT", (b - 1, e))
                for t in range(CH):
                    nc.vector.tensor_scalar(y_sb[e][:, t, :], x1[e][:, t, :], mve[:, t, 0:1], chain[5][:, t:t + 1],
                                            ALU.subtract, ALU.mult).then_inc(e_out, 1)

            dve.wait_ge(econst, 4)
            nc.vector.tensor_scalar(pcode, pcode, PBITS, None, ALU.logical_shift_left).then_inc(pcd, 1)

            def bits(ap):
                return ap.bitcast(I32)

            steps = Steps(dve, dve_step)

            def search(tile, h):
                if h == 0:
                    sim_taken(dve, tile)
                    at_least(dve, cix, tile)
                    nc.vector.tensor_copy(gate[:, 0:1], gate[:, 1:2])
                s, i = s16, i16.bitcast(U32)
                src = [sim[:, (2 * h + c) * NK:(2 * h + c + 1) * NK] for c in range(2)]
                top = [steps.count(nc.vector.max(s[:, h, c, 0:8], src[c])) for c in range(2)]
                for c in range(2):
                    steps.after(top[c])
                    steps.count(nc.vector.max_index(i[:, h, c, 0:8], s[:, h, c, 0:8], src[c]))
                cut = [steps.count(nc.vector.match_replace(left[c], s[:, h, c, 0:8], src[c], GONE)) for c in range(2)]
                top = []
                for c in range(2):
                    steps.after(cut[c])
                    top.append(steps.count(nc.vector.max(s[:, h, c, 8:16], left[c])))
                steps.after(top[0])
                steps.count(nc.vector.max_index(i[:, h, 0, 8:16], s[:, h, 0, 8:16], left[0]))
                steps.after(top[1])
                nc.vector.max_index(i[:, h, 1, 8:16], s[:, h, 1, 8:16], left[1]).then_inc(st1, 1)

            def candidates():
                steps.all()
                s = s16
                for a, rows, n, at in SEGS:
                    o = cand[:, :, at:at + rows * n].rearrange("p h (a b) -> p h a b", a=rows)
                    i0 = s[:, :, 0, a:a + rows].unsqueeze(3).to_broadcast([P, FH, rows, n])
                    i1 = s[:, :, 1, 0:n].unsqueeze(2).to_broadcast([P, FH, rows, n])
                    if rows == 1:
                        o, i0, i1 = o[:, :, 0, :], i0[:, :, 0, :], i1[:, :, 0, :]
                    steps.count(nc.vector.tensor_tensor(o, i0, i1, ALU.add))

            def choose(s):
                hs = (2 * s, 2 * s + 1)
                if s == 0:
                    steps.all()
                a = [steps.count(nc.vector.max(best[:, h, 0:8], cand[:, h, :])) for h in hs]
                b = []
                for n, h in enumerate(hs):
                    steps.after(a[n])
                    b.append(steps.count(nc.vector.match_replace(c1[:, h, :], best[:, h, 0:8], cand[:, h, :], GONE)))
                c = []
                for n, h in enumerate(hs):
                    steps.after(b[n])
                    c.append(steps.count(nc.vector.max(best[:, h, 8:16], c1[:, h, :])))
                for n, h in enumerate(hs):
                    steps.after(c[n])
                    steps.count(nc.vector.match_replace(c1[:, h, :], best[:, h, 8:16], c1[:, h, :], GONE))

            def make_keys(v):
                w, ik = bits(wkey), bits(ikey)
                relu = steps.count(nc.vector.tensor_scalar(wkey, cand, 0.0, 0.0, ALU.max, ALU.add))
                steps.after(relu)
                low = steps.count(nc.vector.tensor_scalar(ik, w, (1 << LOW) - 1, 12, ALU.bitwise_and,
                                                          ALU.logical_shift_left))
                high = steps.count(nc.vector.scalar_tensor_tensor(w, w, LOW, pcode, ALU.logical_shift_right,
                                                                  ALU.bitwise_or))
                dve.wait_ge(cix, v + 1)
                steps.after(low)
                nc.vector.tensor_tensor(ik, ik, cidx, ALU.bitwise_or).then_inc(key, 1)
                steps.after(high)
                steps.count(nc.vector.scalar_tensor_tensor(wkey, c1, GONE, wkey, ALU.is_equal, ALU.mult))
                dve.wait_ge(key, v + 1)
                steps.count(nc.vector.scalar_tensor_tensor(ikey, c1, GONE, ikey, ALU.is_equal, ALU.mult))

            def extract(s):
                if s == 0:
                    steps.all()
                both = [(k, o, h) for h in (2 * s, 2 * s + 1) for k, o in ((wkey, kA), (ikey, kB))]
                a = [steps.count(nc.vector.max(o[:, h, 0:8], k[:, h, :])) for k, o, h in both]
                b = []
                for n, (k, o, h) in enumerate(both):
                    steps.after(a[n])
                    b.append(steps.count(nc.vector.match_replace(k[:, h, :], o[:, h, 0:8], k[:, h, :], 0.0)))
                for n, (k, o, h) in enumerate(both):
                    steps.after(b[n])
                    steps.count(nc.vector.max(o[:, h, 8:16], k[:, h, :]))

            def decode(v):
                a = bits(kA.rearrange("p h n -> p (h n)"))
                b = bits(kB.rearrange("p h n -> p (h n)"))
                at_least(dve, wsp, v)
                tok_filled(dve, v - 1)
                steps.all()
                wa = steps.count(nc.vector.tensor_scalar(wA, a, (1 << PBITS) - 1, LOW, ALU.bitwise_and,
                                                         ALU.logical_shift_left))
                wb = steps.count(nc.vector.tensor_scalar(wB, b, 12, (1 << LOW) - 1, ALU.logical_shift_right,
                                                         ALU.bitwise_and))
                eh = steps.count(nc.vector.tensor_scalar(eH, b, NE - 1, 5, ALU.bitwise_and, ALU.logical_shift_right))
                el = steps.count(nc.vector.tensor_scalar(eL, b, JL - 1, None, ALU.bitwise_and))
                steps.after(wb)
                nc.vector.tensor_tensor(bits(wf), wA, wB, ALU.bitwise_or).then_inc(dec_w, 1)
                steps.after(el)
                steps.count(nc.vector.tensor_copy(tok[:, 0, :], eH))
                nc.vector.tensor_copy(tok[:, 1, :], eL).then_inc(dec, 1)

            def choose_experts(tile, kind, i):
                if kind == "search":
                    search(tile, i)
                elif kind == "candidates":
                    candidates()
                elif kind == "choose":
                    choose(i)
                elif kind == "keys":
                    make_keys(tile)
                else:
                    extract(i)
                    if i == 3:
                        decode(tile)

            def split_first(n):
                f, c, done = proj[n % 2], part[n % 2], 4 * (n // 2)
                wait_taken(dve, "proj", (0, n))
                if n >= 2:
                    dve.wait_ge(part_wr[n - 2], 16)
                nc.vector.tensor_copy(c[:, 0, :], f).then_inc(split_own, 1)
                dve.wait_ge(split_own, done + 1)
                nc.vector.tensor_tensor(rest_own, f, c[:, 0, :], ALU.subtract).then_inc(split_own, 1)
                dve.wait_ge(split_own, done + 2)
                nc.vector.tensor_copy(c[:, 1, :], rest_own).then_inc(split_own, 1)
                dve.wait_ge(split_own, done + 3)
                nc.vector.tensor_tensor(c[:, 2, :], rest_own, c[:, 1, :], ALU.subtract).then_inc(split_own, 1)

            first_norm(0)
            first_norm_apply(0)
            split_first(1)
            split_first(3)
            for g in range(SLOTS):
                b, r = g // HG, g % HG
                for i in range(16):
                    if i == 0 and 1 <= g <= NG:
                        max_parts(g - 1)
                    if g < NG:
                        n = 16 * g + i
                        dve.wait_ge(s_full, n + 1)
                        nc.vector.tensor_reduce(nmx[g % 2][:, i % TB, i // TB:i // TB + 1], psum[n % 3][:, :], AX.X,
                                                ALU.max, negate=True).then_inc(s_max, 1)
                    if i == 3 and r == 0 and b + 1 < B:
                        first_norm(b + 1)
                    if i == 8 and r == 0 and b + 1 < B:
                        first_norm_apply(b + 1)
                    if i == 4 and 3 <= g < NG + 3:
                        normalise(g - 3)
                    if r == 2 and b >= 1 and i in (12, 14):
                        residual(b - 1, (i - 12) // 2)
                    if r == 2 and b >= 1 and i in (13, 15):
                        second_norm(b - 1, (i - 13) // 2)
                    for tile, kind, n in choice.get((g, i), []):
                        if (kind, n) == ("search", 0):
                            steps.restart()
                        choose_experts(tile, kind, n)
            dve.wait_ge(e_out, 4 * B)
            dve.sem_inc(phase, 1)
            dve.wait_ge(phase, 5)

            def one_hots(k, par, kk, q):
                c, r = (k + 1) * 16 + q, 2 * (1 - par) + q // BPT
                if kk == -1 and q == 0:
                    dve.wait_ge(iconst, 2)
                if q % BPT == 0:
                    dve.wait_ge(tokT_ld[r], ((k + 1) * 2 + q // BPT) * 4 + (16 - 4 * r))
                at_least(dve, c_mm, c - 1)
                block_weighed(dve, c - 2)
                t0 = q % BPT * TK
                tt = tokT[r]
                nc.vector.tensor_tensor(oj[q % 2], tt[:, 1:2, t0:t0 + TK].to_broadcast([P, JL, TK]), iota[:, 0:JL, :],
                                        ALU.is_equal).then_inc(oh_rdy, 1)
                nc.vector.tensor_tensor(oh[q % 2], tt[:, 0:1, t0:t0 + TK].to_broadcast([P, P, TK]), iota,
                                        ALU.is_equal).then_inc(oh_rdy, 1)
                if kk == -1 and q in OWN:
                    dve.wait_ge(oh_rdy, c * 2 + 1)
                    i0 = oj[q % 2].unsqueeze(1).to_broadcast([P, 3, JL, TK])
                    i1 = tt[:, 2:5, t0:t0 + TK].unsqueeze(2).to_broadcast([P, 3, JL, TK])
                    nc.vector.tensor_tensor(ow[q % 2], i0, i1, ALU.mult).then_inc(ow_own, 1)

            def weigh_hidden(k, par, q):
                dve.wait_ge(g_act, k * 16 + (q + 1))
                if q == 0:
                    dve.wait_ge(c_ev, (k + 1) * 16)
                nc.vector.tensor_tensor(gm[q % 4], gm[q % 4], coef[par][:, 2 * q:2 * q + 2, :], ALU.mult)\
                  .then_inc(m_rdy, 1)

            def add_residual(k):
                dve.wait_ge(fin_mm, k)
                dve.wait_ge(xr_ld, k * 16)
                nc.vector.tensor_tensor(xr, psum[1][:, :].rearrange("p (t d) -> p t d", t=CH), xr, ALU.add)\
                  .then_inc(fin_add, 1)

            def run(*where):
                for q, k, par, kk, now in walk(*where):
                    k1, p1, kk1, q1 = back(k, par, kk, q, 1)
                    if on(kk1, 0, 7):
                        weigh_hidden(k1, p1, q1)
                    if on(kk, -1, 6):
                        one_hots(k, par, kk, q)
                    for task in now["tasks"]:
                        choose_experts(*task)
                    if q == 4 and on(kk, 1, 8):
                        add_residual(k)
                steps.restart()

            steps.restart()
            runs(dve, run)

        @block.tensor
        def _(pe):
            def mm(o, l, r, first=True, last=True):
                return nc.tensor.matmul(o, l, r, start=first, stop=last)

            def turn(o, i, ident):
                return nc.tensor.transpose(o, i, ident)

            def event(name, index):
                bank, n, ps = place(name, index)
                if n:
                    pe.wait_ge(misc_read[bank], n)
                if name in ("xT", "cT"):
                    b, e = index
                    if name == "xT":
                        pe.wait_ge(ln_out, 4 * (b + 1))
                    else:
                        pe.wait_ge(c_ld[b % 2], 16 * (b // 2 + 1))
                    src = xn_sb if name == "xT" else c_sb[b % 2]
                    for k in range(KD):
                        for t in range(CH):
                            last = turn(ps[:, k * TC + t * P:k * TC + (t + 1) * P],
                                        src[:, e * CH + t, k * P:(k + 1) * P], identf)
                elif name == "proj":
                    b, n4 = index
                    wait_taken(pe, "cT" if n4 % 2 else "xT", (b, 0))
                    wait_taken(pe, "cT" if n4 % 2 else "xT", (b, 1))
                    w, src = (Wk_sb, cT) if n4 % 2 else (Wq_sb, xT)
                    for k in range(KD):
                        last = mm(ps[:, :], w[:, k, n4 // 2 * P:(n4 // 2 + 1) * P], src[:, k, :], k == 0, k == KD - 1)
                elif name == "v":
                    b, e = index
                    wait_taken(pe, "cT", (b, e))
                    for t in range(CH):
                        o = ps[:, t * D:(t + 1) * D]
                        for k in range(KD):
                            mm(o, cT[:, k, (e * CH + t) * P:(e * CH + t + 1) * P], Wv_sb[:, k, :], k == 0, False)
                        last = mm(o, ones[0:1, :], brow[0:1, 0:D], False, True)
                elif name == "max":
                    g = index
                    pe.wait_ge(mp_done, 3 * (g + 1))
                    psb = ps[:, 0:S // 2].bitcast(BF16)
                    for t in range(TB):
                        last = turn(psb[0:MR * HG, t * P:(t + 1) * P], mpart[g % 2][:, t].rearrange("p c h -> p (c h)"), identb)
                elif name == "oT":
                    g = index
                    pe.wait_ge(o_ev, g + 1)
                    for t in range(TB):
                        last = turn(ps[:, t * P:(t + 1) * P], oT[g % 2][:, t * P:(t + 1) * P], identf)
                elif name == "aT":
                    b, e = index
                    wait_taken(pe, "oT", HG * b + 2)
                    wait_taken(pe, "oT", HG * b + 3)
                    for k in range(KD):
                        for t in range(CH):
                            last = turn(ps[:, k * TC + t * P:k * TC + (t + 1) * P],
                                        attn[:, e * CH + t, k * P:(k + 1) * P], identf)
                elif name == "o":
                    b, e = index
                    wait_taken(pe, "aT", (b, e))
                    for t in range(CH):
                        o = ps[:, t * D:(t + 1) * D]
                        for k in range(KD):
                            mm(o, aT[:, k, (e * CH + t) * P:(e * CH + t + 1) * P], Wo_sb[:, k, :], k == 0, False)
                        last = mm(o, ones[0:1, :], brow[0:1, D:2 * D], False, True)
                elif name == "yT":
                    b, e = index
                    pe.wait_ge(e_out, 2 * (2 * b + e + 1))
                    for k in range(KD):
                        for t in range(CH):
                            last = turn(ps[:, k * TC + t * P:k * TC + (t + 1) * P], y_sb[e][:, t, k * P:(k + 1) * P], identf)
                elif name == "down":
                    n2 = index
                    pe.wait_ge(dn_ld[n2 % 2], 16 * (n2 // 2 + 1))
                    for k in range(KD):
                        for j in range(2):
                            last = turn(ps[:, (k * 2 + j) * P:(k * 2 + j + 1) * P],
                                        dn_sb[n2 % 2][:, j, k * P:(k + 1) * P], identf)
                elif name == "wqT":
                    n2 = index
                    pe.wait_ge(wq_ld[n2 % 2], 32 * (n2 // 2 + 1))
                    for c in range(2):
                        for k in range(KD):
                            last = turn(ps[:, (c * KD + k) * P:(c * KD + k + 1) * P],
                                        wq_sb[n2 % 2][:, k, c * P:(c + 1) * P], identf)
                elif name == "kyT":
                    n2 = index
                    for c in range(2):
                        last = turn(ps[:, c * NK:(c + 1) * NK], ky_sb[n2 % 2][0:NK, c, :], identf[0:NK, 0:NK])
                elif name == "wqk":
                    wait_taken(pe, "wqT", index)
                    wait_taken(pe, "kyT", index)
                    for k in range(KD):
                        for c in range(2):
                            last = mm(ps[:, (k * 2 + c) * NK:(k * 2 + c + 1) * NK], wqT[:, c, k, :], kyT[:, c, :])
                elif name == "sim":
                    tile, n = index
                    if tile == 0 and n == 0:
                        wait_taken(pe, "wqk", HP // 2 - 1)
                    if n == 0:
                        pe.wait_ge(xs_ld, 16 * (tile + 1))
                    for k in range(KD):
                        last = mm(ps[:, :], xs[:, k, :], wqk[:, k, n * 512:(n + 1) * 512], k == 0, k == KD - 1)
                elif name == "tok":
                    pe.wait_ge(dec, index + 1)
                    pe.wait_ge(wsp, index + 1)
                    psb = ps[:, 0:5 * P // 2].bitcast(BF16)
                    for c in range(5):
                        last = turn(psb[:, c * P:(c + 1) * P], tok[:, c, :], identb)
                last.then_inc(misc_full[bank], 1)

            def scores(g, i):
                n = 16 * g + i
                if i == 0:
                    pe.wait_ge(st_ld[g % 4], 2 * NSLOT * 16 * (g // 4 + 1))
                if n >= 3:
                    pe.wait_ge(s_max, n - 2)
                hh, t = i // TB, i % TB
                mm(psum[n % 3][:, :], qst[g % 4][0:SK, hh, t * P:(t + 1) * P], kst[g % 4][0:SK, hh, :]).then_inc(s_full, 1)

            def turned_scores(g, i):
                n = 16 * g + i
                if i == 0:
                    pe.wait_ge(mr_ld[g % 4], 16 * (g // 4 + 1))
                if n >= 2:
                    pe.wait_ge(p_ready, n - 1)
                t, hh = i // HG, i % HG
                mm(psum[3 + n % 2][:, :], kst[g % 4][0:SK + MR, hh, t * P:(t + 1) * P], qst[g % 4][0:SK + MR, hh, :])\
                    .then_inc(t_full, 1)

            def values(quad):
                g, t = quad // TB, quad % TB
                b, r = g // HG, g % HG
                pe.wait_ge(p_ready, 4 * (quad + 1))
                if t == 0:
                    if g:
                        pe.wait_ge(o_ev, g)
                    wait_taken(pe, "v", (b, 0))
                    wait_taken(pe, "v", (b, 1))
                for hh in range(HG):
                    last = mm(psum[5][32 * hh:32 * hh + 32, :], v_sb[b % 2][:, t, r * HG + hh, :], p_sb[quad % 3][:, hh, :],
                              t == 0, t == TB - 1)
                last.then_inc(pv_done, 1)

            pe.wait_ge(consts, 11)
            pe.wait_ge(w_ld, 12 * 16)
            for _, name, index in before:
                event(name, index)
            for g in range(SLOTS):
                for i in range(16):
                    for _, name, index in [e for e in plan[g] if e[0] == i]:
                        event(name, index)
                    if 2 <= g < NG + 2:
                        turned_scores(g - 2, i)
                    if g < NG:
                        scores(g, i)
                    quad = 4 * (g - 2) + i // 4 - 1
                    if i % 4 == 1 and 0 <= quad < 4 * NG:
                        values(quad)
            wait_filled(pe, "yT", (B - 1, 1))
            pe.sem_inc(phase, 1)
            pe.wait_ge(phase, 5)

            def similarities(tile, n):
                if n == 0:
                    pe.wait_ge(xs_ld, tile * 16 + 16)
                at_least(pe, sim_ev, tile * 2 + (n - 2 * NA))
                for k in range(KD):
                    last = mm(psum[0][:, :], xs[:, k, :], wqk[:, k, n * 512:(n + 1) * 512], k == 0, k == KD - 1)
                last.then_inc(sim_mm, 1)

            def turn_numbers(tile, k, q):
                pe.wait_ge(dec, tile + 1)
                pe.wait_ge(wsp, tile + 1)
                at_least(pe, tok_ev, tile - NA)
                at_least(pe, fin_add, k - 1 if q <= 3 else k)
                psb = psum[1][:, 0:5 * P // 2].bitcast(BF16)
                for c in range(5):
                    last = turn(psb[:, c * P:(c + 1) * P], tok[:, c, :], identb)
                last.then_inc(tok_mm, 1)

            def coefficients(k, q):
                c = (k + 1) * 16 + q
                pe.wait_ge(oh_rdy, c * 2 + 2)
                block_weighed(pe, c)
                at_least(pe, c_ev, c - 1)
                for t in range(TK):
                    for w in range(3):
                        last = mm(psum[2 + q % 2][:, t * JL:(t + 1) * JL], oh[q % 2][:, :, t], ow[q % 2][:, w, :, t],
                                  w == 0, w == 2)
                last.then_inc(c_mm, 1)

            def hidden(k, kk, par, q):
                if kk == 0 and q % 4 == 0:
                    pe.wait_ge(dt_ld[q // 4], 16)
                if q == 0:
                    pe.wait_ge(xm_ld[par], (k - par) * 8 + 16)
                at_least(pe, g_act, k * 16 + (q - 1))
                for j in range(2):
                    for c in range(KD):
                        last = mm(psum[4 + q % 2][:, j * TC:(j + 1) * TC], downT[:, c, 2 * q + j, :], xm[par][:, c, :],
                                  c == 0, c == KD - 1)
                last.then_inc(g_mm, 1)

            def output(k, kk, q):
                if kk == 0 and q % 4 == 0:
                    pe.wait_ge(up_ld[q // 4], 16)
                if q == 0:
                    at_least(pe, ot_ev, k)
                pe.wait_ge(m_rdy, k * 16 + (q + 1))
                for j in range(2):
                    for c in range(KD):
                        last = mm(psum[6 + c][:, 0:TC], up_sb[:, 2 * q + j, c * P:(c + 1) * P], gm[q % 4][:, j, :],
                                  q == 0 and j == 0, q == 15 and j == 1)
                last.then_inc(o_mm, 1)

            def turn_output(k, turned):
                pe.wait_ge(ot_ev, k)
                at_least(pe, tok_ev, turned - (NA - 1))
                at_least(pe, fin_add, k - 1)
                for t in range(CH):
                    for c in range(KD):
                        last = turn(psum[1][:, t * D + c * P:t * D + (c + 1) * P], outT[:, c, t * P:(t + 1) * P], identf)
                last.then_inc(fin_mm, 1)

            similarities(NA, 0)
            similarities(NA, 1)

            def run(*where):
                for q, k, par, kk, now in walk(*where):
                    if on(kk, 0, 7):
                        hidden(k, kk, par, q)
                    k1, p1, kk1, q1 = back(k, par, kk, q, 1)
                    if on(kk1, -1, 6):
                        coefficients(k1, q1)
                    k2, p2, kk2, q2 = back(k, par, kk, q, 2)
                    if on(kk2, 0, 7):
                        output(k2, kk2, q2)
                    for tile in now["turn"]:
                        turn_numbers(tile, k, q)
                    if q == 3 and on(kk, 1, 8):
                        turn_output(k, now["turned"])
                    for tile, n in now["mult"]:
                        similarities(tile, n)

            runs(pe, run)


_INS = ["x", "ctx_1024", "L0_xattn_Wq", "L0_xattn_bq", "L0_xattn_Wk", "L0_xattn_bk", "L0_xattn_Wv", "L0_xattn_bv",
        "L0_xattn_Wo", "L0_xattn_bo", "L0_ffn_norm_w", "L0_ffn_wq", "L0_ffn_keys", "L0_ffn_expert_down",
        "L0_ffn_expert_up"]


def kernel(**inputs):
    import concourse.bacc as bacc
    from concourse.bass_utils import run_bass_kernel_spmd

    nc = bacc.Bacc("TRN2", target_bir_lowering=False, num_devices=1)
    arrays, args = {}, []
    for name in _INS:
        a = np.ascontiguousarray(inputs[name])
        arrays[f"in_{name}"] = a
        args.append(nc.dram_tensor(f"in_{name}", a.shape, mybir.dt.from_np(a.dtype), kind="ExternalInput").ap())
    out = nc.dram_tensor("out_0", (B, S, D), F32, kind="ExternalOutput").ap()
    build(nc, *args, out)
    r = run_bass_kernel_spmd(nc, [arrays], core_ids=[0])
    return r.results[0]["out_0"]
```
